# Optimizing a Trainium2 kernel written in Bass

```python
import numpy as np
import jax
import jax.numpy as jnp

def _softmax(x, axis=-1):
    return jax.nn.softmax(x, axis=axis)

def _gelu(x):
    return jax.nn.gelu(x, approximate=True)

def _silu(x):
    return jax.nn.silu(x)

def _sigmoid(x):
    return jax.nn.sigmoid(x)

def _layernorm(x, axis=-1, eps=1e-05):
    m = jnp.mean(x, axis=axis, keepdims=True)
    v = jnp.var(x, axis=axis, keepdims=True)
    return (x - m) / jnp.sqrt(v + eps)

def _scatter_add(tgt, idx, src, axis=0):
    return tgt.at[idx].add(src)

def _segment_sum(src, seg, n):
    return jax.ops.segment_sum(src, seg, n)
kernel_name = 'mk_adj_ffn_d4_adj_r2_86b6fa'

def setup_inputs(seed: int=0):
    np.random.seed(seed)
    _w = jnp.asarray

    def _rec_inputs():
        import jax
        import jax.numpy as jnp
        _gk = jax.random.key(seed)
        x = -0.0002928 + 1 * jax.random.normal(jax.random.fold_in(_gk, 1), (1354, 256), jnp.float32)
        _a = jax.random.bernoulli(jax.random.fold_in(_gk, 2), 0.0014771, (1354, 1354))
        _a = jnp.logical_or(_a, jnp.eye(1354, dtype=bool))
        _af = _a.astype(jnp.float32)
        _af = _af * jax.random.uniform(jax.random.fold_in(_gk, 3), (1354, 1354), jnp.float32, 0.05, 1)
        adj = _af
        return (x, adj)
    x, adj = _rec_inputs()

    def _L0_gnn_setup():
        import jax, jax.numpy as jnp
        import numpy as np
        N = 4096
        DIN = 256
        DOUT = 256
        key = jax.random.key(seed)
        k1, k2, k3 = jax.random.split(key, 3)
        x = jax.random.normal(k1, (N, DIN), dtype=jnp.float32)
        adj = jax.random.uniform(k2, (N, N), dtype=jnp.float32)
        W = jax.random.normal(k3, (DIN, DOUT), dtype=jnp.float32) * (1.0 / np.sqrt(DIN))
        b = jnp.zeros((DOUT,), dtype=jnp.float32)
        return {'x': x, 'adj': adj, 'W': W, 'b': b}
    _L0_gnn_all = _L0_gnn_setup()
    _L0_gnn_in = {k: v for k, v in _L0_gnn_all.items() if k in ('W', 'b')}
    del _L0_gnn_all

    def _L0_ffn_setup():
        import jax, jax.numpy as jnp
        import numpy as np
        B, S, D, H, O, E, TOPK = (4, 1024, 256, 512, 256, 8, 2)
        key = jax.random.key(seed)
        ks = jax.random.split(key, 6)
        s = lambda d: 1.0 / np.sqrt(d)
        return {'x': jax.random.normal(ks[0], (B, S, D), dtype=jnp.float32), 'Wg': jax.random.normal(ks[1], (D, E), dtype=jnp.float32) * s(D), 'W1': jax.random.normal(ks[2], (E, D, H), dtype=jnp.float32) * s(D), 'b1': jnp.zeros((E, H), dtype=jnp.float32), 'W2': jax.random.normal(ks[3], (E, H, O), dtype=jnp.float32) * s(H), 'b2': jnp.zeros((E, O), dtype=jnp.float32)}
    _L0_ffn_all = _L0_ffn_setup()
    _L0_ffn_in = {k: v for k, v in _L0_ffn_all.items() if k in ('Wg', 'W1', 'b1', 'W2', 'b2')}
    del _L0_ffn_all

    def _L1_gnn_setup():
        import jax, jax.numpy as jnp
        import numpy as np
        N = 4096
        D = 256
        EPS = 1e-12
        key = jax.random.key(seed)
        k1, k2 = jax.random.split(key)
        cur = jax.random.normal(k1, (N, D), dtype=jnp.float32)
        incidence_m = jax.random.normal(k2, (N, N), dtype=jnp.float32)
        return {'cur': cur, 'incidence_m': incidence_m}
    _L1_gnn_all = _L1_gnn_setup()
    _L1_gnn_in = {k: v for k, v in _L1_gnn_all.items() if k in ()}
    del _L1_gnn_all

    def _L1_ffn_setup():
        import jax, jax.numpy as jnp
        import numpy as np
        B, S, D, F, E, NS, K = (2, 1024, 256, 1024, 8, 2, 2)
        key = jax.random.key(seed)
        ks = jax.random.split(key, 6)
        scale = 0.02

        def p(k, shape):
            return jax.random.normal(k, shape, jnp.float32) * scale
        return {'x': jax.random.normal(ks[0], (B, S, D), jnp.float32), 'gate_w': p(ks[1], (E, D)), 'gate_b': jnp.zeros((E,), jnp.float32), 'sw1': p(ks[2], (NS, F, D)), 'sb1': jnp.zeros((NS, F), jnp.float32), 'sw2': p(ks[3], (NS, D, F)), 'sb2': jnp.zeros((NS, D), jnp.float32), 'rw1': p(ks[4], (E, F, D)), 'rb1': jnp.zeros((E, F), jnp.float32), 'rw2': p(ks[5], (E, D, F)), 'rb2': jnp.zeros((E, D), jnp.float32)}
    _L1_ffn_all = _L1_ffn_setup()
    _L1_ffn_in = {k: v for k, v in _L1_ffn_all.items() if k in ('gate_w', 'gate_b', 'sw1', 'sb1', 'sw2', 'sb2', 'rw1', 'rb1', 'rw2', 'rb2')}
    del _L1_ffn_all

    def _L2_gnn_setup():
        import jax, jax.numpy as jnp
        import numpy as np
        N = 2048
        D = 256
        H = 4
        NEG = -10000000000.0
        ALPHA = 0.3
        key = jax.random.key(seed)
        ks = jax.random.split(key, 8)
        nodes = jax.random.normal(ks[0], (N, D), dtype=jnp.float32)
        adj = (jax.random.uniform(ks[1], (N, N)) < 0.01).astype(jnp.float32)
        adj = jnp.maximum(adj, jnp.eye(N, dtype=jnp.float32))
        s = 0.05
        W_node = jax.random.normal(ks[2], (D, D), dtype=jnp.float32) * s
        b_node = jnp.zeros((D,), dtype=jnp.float32)
        K = jax.random.normal(ks[3], (H, D, D), dtype=jnp.float32) * s
        A_self = jax.random.normal(ks[4], (H, D), dtype=jnp.float32) * s
        A_neigh = jax.random.normal(ks[5], (H, D), dtype=jnp.float32) * s
        return {'nodes': nodes, 'adj': adj, 'W_node': W_node, 'b_node': b_node, 'K': K, 'A_self': A_self, 'A_neigh': A_neigh, 'num_heads': H}
    _L2_gnn_all = _L2_gnn_setup()
    _L2_gnn_in = {k: v for k, v in _L2_gnn_all.items() if k in ('W_node', 'b_node', 'K', 'A_self', 'A_neigh')}
    del _L2_gnn_all

    def _L2_ffn_setup():
        import jax, jax.numpy as jnp
        import numpy as np
        from jax import lax
        B, L = (4, 512)
        D_MODEL, D_STATE, D_CONV = (256, 16, 4)
        D_INNER = 2 * D_MODEL
        DT_RANK = D_MODEL // 16
        K_EXPERTS = 2
        EPS = 1e-05

        def _layernorm(x):
            mu = jnp.mean(x, -1, keepdims=True)
            var = jnp.mean(jnp.square(x - mu), -1, keepdims=True)
            return (x - mu) / jnp.sqrt(var + EPS)

        def _mamba(x, in_proj_w, conv_w, conv_b, x_proj_w, dt_proj_w, dt_proj_b, A_log, D_skip, out_proj_w):
            b = x.shape[0]
            xz = x @ in_proj_w.T
            xc, z = jnp.split(xz, 2, axis=-1)
            conv = lax.conv_general_dilated(xc.transpose(0, 2, 1), conv_w, (1,), [(D_CONV - 1, 0)], feature_group_count=D_INNER) + conv_b[None, :, None]
            xs = jax.nn.silu(conv).transpose(0, 2, 1)
            dbc = xs @ x_proj_w.T
            dt = dbc[..., :DT_RANK]
            Bm = dbc[..., DT_RANK:DT_RANK + D_STATE]
            Cm = dbc[..., DT_RANK + D_STATE:]
            delta = jax.nn.softplus(dt @ dt_proj_w.T + dt_proj_b)
            A = -jnp.exp(A_log)
            dA = jnp.exp(jnp.einsum('bld,dn->bldn', delta, A))
            dBx = (delta * xs)[..., None] * Bm[:, :, None, :]

            def step(h, inp):
                dA_t, dBx_t, C_t = inp
                h = dA_t * h + dBx_t
                y = jnp.einsum('bdn,bn->bd', h, C_t)
                return (h, y)
            h0 = jnp.zeros((b, D_INNER, D_STATE), x.dtype)
            _, ys = lax.scan(step, h0, (dA.transpose(1, 0, 2, 3), dBx.transpose(1, 0, 2, 3), Cm.transpose(1, 0, 2)))
            y = ys.transpose(1, 0, 2) + xs * D_skip
            y = y * jax.nn.silu(z)
            return y @ out_proj_w.T
        key = jax.random.key(seed)
        ks = jax.random.split(key, 14)

        def n(k, shape, scale=0.02):
            return jax.random.normal(k, shape, jnp.float32) * scale
        A_log = jnp.log(jnp.broadcast_to(jnp.arange(1, D_STATE + 1, dtype=jnp.float32), (D_INNER, D_STATE)))
        return {'x': jax.random.normal(ks[0], (B, L, D_MODEL), jnp.float32), 'in_proj_w': n(ks[1], (2 * D_INNER, D_MODEL)), 'conv_w': n(ks[2], (D_INNER, 1, D_CONV), 0.1), 'conv_b': n(ks[3], (D_INNER,), 0.1), 'x_proj_w': n(ks[4], (DT_RANK + 2 * D_STATE, D_INNER)), 'dt_proj_w': n(ks[5], (D_INNER, DT_RANK), 0.1), 'dt_proj_b': n(ks[6], (D_INNER,), 0.1), 'A_log': A_log, 'D_skip': jnp.ones((D_INNER,), jnp.float32), 'out_proj_w': n(ks[7], (D_MODEL, D_INNER)), 'moe_w1': n(ks[8], (K_EXPERTS, 2 * D_MODEL, D_MODEL)), 'moe_b1': n(ks[9], (K_EXPERTS, 2 * D_MODEL)), 'moe_w2': n(ks[10], (K_EXPERTS, D_MODEL, 2 * D_MODEL)), 'moe_b2': n(ks[11], (K_EXPERTS, D_MODEL))}
    _L2_ffn_all = _L2_ffn_setup()
    _L2_ffn_in = {k: v for k, v in _L2_ffn_all.items() if k in ('in_proj_w', 'conv_w', 'conv_b', 'x_proj_w', 'dt_proj_w', 'dt_proj_b', 'A_log', 'D_skip', 'out_proj_w', 'moe_w1', 'moe_b1', 'moe_w2', 'moe_b2')}
    del _L2_ffn_all

    def _L3_gnn_setup():
        import jax, jax.numpy as jnp
        import numpy as np
        N = 3072
        D_IN = 256
        D_OUT = 256
        DENSITY = 0.005
        key = jax.random.key(seed)
        ks = jax.random.split(key, 12)
        x = jax.random.normal(ks[0], (N, D_IN), dtype=jnp.float32)
        adj_a = (jax.random.uniform(ks[1], (N, N)) < DENSITY).astype(jnp.float32)
        adj_b = (jax.random.uniform(ks[2], (N, N)) < DENSITY).astype(jnp.float32)
        W_sa = jax.random.normal(ks[3], (D_IN, D_OUT), dtype=jnp.float32) * (1.414 / np.sqrt(D_IN + D_OUT))
        a_sa = jax.random.normal(ks[4], (1, 2 * D_OUT), dtype=jnp.float32) * (1.414 / np.sqrt(1 + 2 * D_OUT))
        stdv = 1.0 / np.sqrt(D_OUT)
        W_gcnb = jax.random.uniform(ks[5], (D_IN, D_OUT), minval=-stdv, maxval=stdv, dtype=jnp.float32)
        b_gcnb = jax.random.uniform(ks[6], (D_OUT,), minval=-stdv, maxval=stdv, dtype=jnp.float32)
        s = 1.0 / np.sqrt(2 * D_IN)
        Wa = jax.random.uniform(ks[7], (1, 2 * D_IN), minval=-s, maxval=s, dtype=jnp.float32)
        ba = jax.random.uniform(ks[8], (1,), minval=-s, maxval=s, dtype=jnp.float32)
        Wb = jax.random.uniform(ks[9], (1, 2 * D_IN), minval=-s, maxval=s, dtype=jnp.float32)
        bb = jax.random.uniform(ks[10], (1,), minval=-s, maxval=s, dtype=jnp.float32)
        return {'x': x, 'adj_a': adj_a, 'adj_b': adj_b, 'W_sa': W_sa, 'a_sa': a_sa, 'W_gcnb': W_gcnb, 'b_gcnb': b_gcnb, 'Wa': Wa, 'ba': ba, 'Wb': Wb, 'bb': bb}
    _L3_gnn_all = _L3_gnn_setup()
    _L3_gnn_in = {k: v for k, v in _L3_gnn_all.items() if k in ('W_sa', 'a_sa', 'W_gcnb', 'b_gcnb', 'Wa', 'ba', 'Wb', 'bb')}
    del _L3_gnn_all

    def _L3_ffn_setup():
        import jax, jax.numpy as jnp
        import numpy as np
        TEMPERATURE = 2.5
        TOPK = 2
        key = jax.random.key(seed)
        ks = jax.random.split(key, 4)
        B, T, D, F, E = (8, 4096, 256, 1024, 8)
        x = jax.random.normal(ks[0], (B, T, D), jnp.float32)
        Wr = jax.random.normal(ks[1], (D, E), jnp.float32) * D ** (-0.5)
        W1 = jax.random.normal(ks[2], (E, D, F), jnp.float32) * D ** (-0.5)
        b1 = jnp.zeros((E, F), jnp.float32)
        W2 = jax.random.normal(ks[3], (E, F, D), jnp.float32) * F ** (-0.5)
        b2 = jnp.zeros((E, D), jnp.float32)
        return {'x': x, 'Wr': Wr, 'W1': W1, 'b1': b1, 'W2': W2, 'b2': b2}
    _L3_ffn_all = _L3_ffn_setup()
    _L3_ffn_in = {k: v for k, v in _L3_ffn_all.items() if k in ('Wr', 'W1', 'b1', 'W2', 'b2')}
    del _L3_ffn_all
    return {'x': x, 'adj': adj, 'L0_gnn_W': _L0_gnn_in['W'], 'L0_gnn_b': _L0_gnn_in['b'], 'L0_ffn_Wg': _L0_ffn_in['Wg'], 'L0_ffn_W1': _L0_ffn_in['W1'], 'L0_ffn_b1': _L0_ffn_in['b1'], 'L0_ffn_W2': _L0_ffn_in['W2'], 'L0_ffn_b2': _L0_ffn_in['b2'], 'L1_ffn_gate_w': _L1_ffn_in['gate_w'], 'L1_ffn_gate_b': _L1_ffn_in['gate_b'], 'L1_ffn_sw1': _L1_ffn_in['sw1'], 'L1_ffn_sb1': _L1_ffn_in['sb1'], 'L1_ffn_sw2': _L1_ffn_in['sw2'], 'L1_ffn_sb2': _L1_ffn_in['sb2'], 'L1_ffn_rw1': _L1_ffn_in['rw1'], 'L1_ffn_rb1': _L1_ffn_in['rb1'], 'L1_ffn_rw2': _L1_ffn_in['rw2'], 'L1_ffn_rb2': _L1_ffn_in['rb2'], 'L2_gnn_W_node': _L2_gnn_in['W_node'], 'L2_gnn_b_node': _L2_gnn_in['b_node'], 'L2_gnn_K': _L2_gnn_in['K'], 'L2_gnn_A_self': _L2_gnn_in['A_self'], 'L2_gnn_A_neigh': _L2_gnn_in['A_neigh'], 'L2_ffn_in_proj_w': _L2_ffn_in['in_proj_w'], 'L2_ffn_conv_w': _L2_ffn_in['conv_w'], 'L2_ffn_conv_b': _L2_ffn_in['conv_b'], 'L2_ffn_x_proj_w': _L2_ffn_in['x_proj_w'], 'L2_ffn_dt_proj_w': _L2_ffn_in['dt_proj_w'], 'L2_ffn_dt_proj_b': _L2_ffn_in['dt_proj_b'], 'L2_ffn_A_log': _L2_ffn_in['A_log'], 'L2_ffn_D_skip': _L2_ffn_in['D_skip'], 'L2_ffn_out_proj_w': _L2_ffn_in['out_proj_w'], 'L2_ffn_moe_w1': _L2_ffn_in['moe_w1'], 'L2_ffn_moe_b1': _L2_ffn_in['moe_b1'], 'L2_ffn_moe_w2': _L2_ffn_in['moe_w2'], 'L2_ffn_moe_b2': _L2_ffn_in['moe_b2'], 'L3_gnn_W_sa': _L3_gnn_in['W_sa'], 'L3_gnn_a_sa': _L3_gnn_in['a_sa'], 'L3_gnn_W_gcnb': _L3_gnn_in['W_gcnb'], 'L3_gnn_b_gcnb': _L3_gnn_in['b_gcnb'], 'L3_gnn_Wa': _L3_gnn_in['Wa'], 'L3_gnn_ba': _L3_gnn_in['ba'], 'L3_gnn_Wb': _L3_gnn_in['Wb'], 'L3_gnn_bb': _L3_gnn_in['bb'], 'L3_ffn_Wr': _L3_ffn_in['Wr'], 'L3_ffn_W1': _L3_ffn_in['W1'], 'L3_ffn_b1': _L3_ffn_in['b1'], 'L3_ffn_W2': _L3_ffn_in['W2'], 'L3_ffn_b2': _L3_ffn_in['b2']}

def reference(x, adj, L0_gnn_W, L0_gnn_b, L0_ffn_Wg, L0_ffn_W1, L0_ffn_b1, L0_ffn_W2, L0_ffn_b2, L1_ffn_gate_w, L1_ffn_gate_b, L1_ffn_sw1, L1_ffn_sb1, L1_ffn_sw2, L1_ffn_sb2, L1_ffn_rw1, L1_ffn_rb1, L1_ffn_rw2, L1_ffn_rb2, L2_gnn_W_node, L2_gnn_b_node, L2_gnn_K, L2_gnn_A_self, L2_gnn_A_neigh, L2_ffn_in_proj_w, L2_ffn_conv_w, L2_ffn_conv_b, L2_ffn_x_proj_w, L2_ffn_dt_proj_w, L2_ffn_dt_proj_b, L2_ffn_A_log, L2_ffn_D_skip, L2_ffn_out_proj_w, L2_ffn_moe_w1, L2_ffn_moe_b1, L2_ffn_moe_w2, L2_ffn_moe_b2, L3_gnn_W_sa, L3_gnn_a_sa, L3_gnn_W_gcnb, L3_gnn_b_gcnb, L3_gnn_Wa, L3_gnn_ba, L3_gnn_Wb, L3_gnn_bb, L3_ffn_Wr, L3_ffn_W1, L3_ffn_b1, L3_ffn_W2, L3_ffn_b2):
    import jax
    import jax.numpy as jnp

    def _L0_gnn_ref(x, adj, W, b):
        import jax, jax.numpy as jnp
        import numpy as np
        N = 4096
        DIN = 256
        DOUT = 256
        rowsum = adj.sum(axis=1)
        d_inv_sqrt = jnp.where(rowsum > 0, rowsum ** (-0.5), 0.0)
        normalized_adj = d_inv_sqrt[:, None] * adj * d_inv_sqrt[None, :]
        support = normalized_adj @ x
        out = support @ W + b
        return jax.nn.relu(out)

    def _L0_ffn_ref(x, Wg, W1, b1, W2, b2):
        import jax, jax.numpy as jnp
        import numpy as np
        B, S, D, H, O, E, TOPK = (4, 1024, 256, 512, 256, 8, 2)
        Bsz, Seq, Din = x.shape
        T = Bsz * Seq
        xm = x.reshape(T, Din)
        probs = jax.nn.softmax(xm @ Wg, axis=-1)
        top_p, top_i = jax.lax.top_k(probs, TOPK)
        gates = jnp.zeros((T, E), dtype=probs.dtype).at[jnp.arange(T)[:, None], top_i].set(top_p)
        h = jax.nn.gelu(jnp.einsum('td,edh->teh', xm, W1) + b1[None])
        y = jnp.einsum('teh,eho->teo', h, W2) + b2[None]
        out = jnp.einsum('te,teo->to', gates, y)
        return out.reshape(Bsz, Seq, O)

    def _L1_gnn_ref(cur, incidence_m):
        import jax, jax.numpy as jnp
        import numpy as np
        N = 4096
        D = 256
        EPS = 1e-12
        mask = incidence_m > 0
        head = jax.lax.stop_gradient(mask.astype(incidence_m.dtype))
        head = head / jnp.maximum(jnp.sqrt(jnp.sum(head * head, axis=-1, keepdims=True)), EPS)
        inc = incidence_m + head
        edge_fea = inc @ cur
        edge_degree = jnp.sum(inc, axis=-1, keepdims=True)
        return edge_fea / edge_degree

    def _L1_ffn_ref(x, gate_w, gate_b, sw1, sb1, sw2, sb2, rw1, rb1, rw2, rb2):
        import jax, jax.numpy as jnp
        import numpy as np
        B, S, D, F, E, NS, K = (2, 1024, 256, 1024, 8, 2, 2)
        b, s, d = x.shape
        t = x.reshape(-1, d)
        T = t.shape[0]
        hs = jax.nn.gelu(jnp.einsum('td,nfd->ntf', t, sw1) + sb1[:, None, :], approximate=False)
        shared = jnp.einsum('ntf,ndf->td', hs, sw2) + sb2.sum(axis=0)
        logits = t @ gate_w.T + gate_b
        probs = jax.nn.softmax(logits, axis=-1)
        top_v, top_i = jax.lax.top_k(probs, K)
        cw = jnp.zeros_like(probs).at[jnp.arange(T)[:, None], top_i].add(top_v)
        hr = jax.nn.gelu(jnp.einsum('td,efd->etf', t, rw1) + rb1[:, None, :], approximate=False)
        oe = jnp.einsum('etf,edf->etd', hr, rw2) + rb2[:, None, :]
        routed = jnp.einsum('etd,te->td', oe, cw)
        return (shared + routed).reshape(b, s, d)

    def _L2_gnn_ref(nodes, adj, W_node, b_node, K, A_self, A_neigh, num_heads):
        import jax, jax.numpy as jnp
        import numpy as np
        N = 2048
        D = 256
        H = 4
        NEG = -10000000000.0
        ALPHA = 0.3
        x = nodes @ W_node + b_node
        feats = jnp.einsum('nd,hdf->hnf', x, K)
        s = jnp.einsum('hnf,hf->hn', feats, A_self) + jnp.einsum('hnf,hf->hn', feats, A_neigh)
        s = jnp.where(s > 0, s, ALPHA * s)
        logits = s[:, :, None] + NEG * (1.0 - adj)[None]
        attn = jax.nn.softmax(logits, axis=-1)
        out = jnp.einsum('hij,hjf->hif', attn, feats)
        out = jnp.mean(out, axis=0)
        return jax.nn.relu(out)

    def _L2_ffn_ref(x, in_proj_w, conv_w, conv_b, x_proj_w, dt_proj_w, dt_proj_b, A_log, D_skip, out_proj_w, moe_w1, moe_b1, moe_w2, moe_b2):
        import jax, jax.numpy as jnp
        import numpy as np
        from jax import lax
        B, L = (4, 512)
        D_MODEL, D_STATE, D_CONV = (256, 16, 4)
        D_INNER = 2 * D_MODEL
        DT_RANK = D_MODEL // 16
        K_EXPERTS = 2
        EPS = 1e-05

        def _layernorm(x):
            mu = jnp.mean(x, -1, keepdims=True)
            var = jnp.mean(jnp.square(x - mu), -1, keepdims=True)
            return (x - mu) / jnp.sqrt(var + EPS)

        def _mamba(x, in_proj_w, conv_w, conv_b, x_proj_w, dt_proj_w, dt_proj_b, A_log, D_skip, out_proj_w):
            b = x.shape[0]
            xz = x @ in_proj_w.T
            xc, z = jnp.split(xz, 2, axis=-1)
            conv = lax.conv_general_dilated(xc.transpose(0, 2, 1), conv_w, (1,), [(D_CONV - 1, 0)], feature_group_count=D_INNER) + conv_b[None, :, None]
            xs = jax.nn.silu(conv).transpose(0, 2, 1)
            dbc = xs @ x_proj_w.T
            dt = dbc[..., :DT_RANK]
            Bm = dbc[..., DT_RANK:DT_RANK + D_STATE]
            Cm = dbc[..., DT_RANK + D_STATE:]
            delta = jax.nn.softplus(dt @ dt_proj_w.T + dt_proj_b)
            A = -jnp.exp(A_log)
            dA = jnp.exp(jnp.einsum('bld,dn->bldn', delta, A))
            dBx = (delta * xs)[..., None] * Bm[:, :, None, :]

            def step(h, inp):
                dA_t, dBx_t, C_t = inp
                h = dA_t * h + dBx_t
                y = jnp.einsum('bdn,bn->bd', h, C_t)
                return (h, y)
            h0 = jnp.zeros((b, D_INNER, D_STATE), x.dtype)
            _, ys = lax.scan(step, h0, (dA.transpose(1, 0, 2, 3), dBx.transpose(1, 0, 2, 3), Cm.transpose(1, 0, 2)))
            y = ys.transpose(1, 0, 2) + xs * D_skip
            y = y * jax.nn.silu(z)
            return y @ out_proj_w.T
        skip = x
        h = _layernorm(x)
        h = _mamba(h, in_proj_w, conv_w, conv_b, x_proj_w, dt_proj_w, dt_proj_b, A_log, D_skip, out_proj_w) + h
        h = _layernorm(h)
        a = jax.nn.relu(jnp.einsum('bld,ekd->belk', h, moe_w1) + moe_b1[None, :, None, :])
        moe = jnp.einsum('belk,edk->beld', a, moe_w2) + moe_b2[None, :, None, :]
        return jnp.mean(moe, axis=1) + skip

    def _L3_gnn_ref(x, adj_a, adj_b, W_sa, a_sa, W_gcnb, b_gcnb, Wa, ba, Wb, bb):
        import jax, jax.numpy as jnp
        import numpy as np
        N = 3072
        D_IN = 256
        D_OUT = 256
        DENSITY = 0.005
        type_sum_a = adj_a @ x
        type_sum_b = adj_b @ x
        attn_a = jax.nn.sigmoid(jnp.concatenate([type_sum_a, x], axis=1) @ Wa.T + ba)
        attn_b = jax.nn.sigmoid(jnp.concatenate([type_sum_b, x], axis=1) @ Wb.T + bb)
        h = x @ W_sa
        Hd = h.shape[1]
        s_left = h @ a_sa[0, :Hd]
        s_right = h @ a_sa[0, Hd:]
        scores = s_left[:, None] + s_right[None, :]
        e = jnp.where(adj_a != 0, jnp.exp(-jax.nn.leaky_relu(scores, 0.01)), 0.0)
        attn = e / (jnp.sum(e, axis=1, keepdims=True) + 1e-05)
        x_a = attn @ h
        x_b = adj_b @ (x @ W_gcnb) + b_gcnb
        return jax.nn.sigmoid(attn_a * x_a + attn_b * x_b)

    def _L3_ffn_ref(x, Wr, W1, b1, W2, b2):
        import jax, jax.numpy as jnp
        import numpy as np
        TEMPERATURE = 2.5
        TOPK = 2
        B, T, D = x.shape
        E = Wr.shape[1]
        N = B * T
        xf = x.reshape(N, D)
        logits = xf @ Wr
        probs = jax.nn.softmax(logits / TEMPERATURE, axis=-1)
        topk_vals, topk_idx = jax.lax.top_k(probs, TOPK)
        topk_vals = topk_vals / jnp.sum(topk_vals, axis=-1, keepdims=True)
        w = jnp.zeros((N, E), xf.dtype)
        w = w.at[jnp.arange(N)[:, None], topk_idx].add(topk_vals)
        out = jnp.zeros_like(xf)
        for e in range(E):
            h = jax.nn.gelu(xf @ W1[e] + b1[e])
            out = out + w[:, e:e + 1] * (h @ W2[e] + b2[e])
        return out.reshape(B, T, D)
    x = x + _L0_gnn_ref(_layernorm(x, axis=-1), adj, L0_gnn_W, L0_gnn_b)
    x = x + _L0_ffn_ref(_layernorm(x, axis=-1)[None], L0_ffn_Wg, L0_ffn_W1, L0_ffn_b1, L0_ffn_W2, L0_ffn_b2)[0]
    x = x + _L1_gnn_ref(_layernorm(x, axis=-1), adj)
    x = x + _L1_ffn_ref(_layernorm(x, axis=-1)[None], L1_ffn_gate_w, L1_ffn_gate_b, L1_ffn_sw1, L1_ffn_sb1, L1_ffn_sw2, L1_ffn_sb2, L1_ffn_rw1, L1_ffn_rb1, L1_ffn_rw2, L1_ffn_rb2)[0]
    x = x + _L2_gnn_ref(_layernorm(x, axis=-1), adj, L2_gnn_W_node, L2_gnn_b_node, L2_gnn_K, L2_gnn_A_self, L2_gnn_A_neigh, 4)
    x = x + _L2_ffn_ref(_layernorm(x, axis=-1)[None], L2_ffn_in_proj_w, L2_ffn_conv_w, L2_ffn_conv_b, L2_ffn_x_proj_w, L2_ffn_dt_proj_w, L2_ffn_dt_proj_b, L2_ffn_A_log, L2_ffn_D_skip, L2_ffn_out_proj_w, L2_ffn_moe_w1, L2_ffn_moe_b1, L2_ffn_moe_w2, L2_ffn_moe_b2)[0]
    x = x + _L3_gnn_ref(_layernorm(x, axis=-1), adj, adj, L3_gnn_W_sa, L3_gnn_a_sa, L3_gnn_W_gcnb, L3_gnn_b_gcnb, L3_gnn_Wa, L3_gnn_ba, L3_gnn_Wb, L3_gnn_bb)
    x = x + _L3_ffn_ref(_layernorm(x, axis=-1)[None], L3_ffn_Wr, L3_ffn_W1, L3_ffn_b1, L3_ffn_W2, L3_ffn_b2)[0]
    return x

_drawn_inputs = setup_inputs


def setup_inputs(seed=0):
    import zlib

    import numpy as np

    out = dict(_drawn_inputs(seed))
    spreads = {'L0_gnn_b': (0.0, 0.1),
     'L0_ffn_b1': (0.0, 0.1),
     'L0_ffn_b2': (0.0, 0.1),
     'L1_ffn_gate_b': (0.0, 0.47),
     'L1_ffn_sb1': (0.0, 0.1),
     'L1_ffn_sb2': (0.0, 0.1),
     'L1_ffn_rb1': (0.0, 0.551),
     'L1_ffn_rb2': (0.0, 0.323),
     'L2_gnn_b_node': (0.0, 0.326),
     'L2_ffn_D_skip': (1.0, 0.6),
     'L3_ffn_b1': (0.0, 0.479),
     'L3_ffn_b2': (0.0, 0.332)}
    factors = {'L2_ffn_in_proj_w': 8.0,
     'L2_ffn_conv_w': 8.0,
     'L2_ffn_conv_b': 22.787,
     'L2_ffn_x_proj_w': 8.0,
     'L2_ffn_dt_proj_w': 8.0,
     'L2_ffn_dt_proj_b': 64.0,
     'L2_ffn_A_log': 27.628,
     'L2_ffn_out_proj_w': 8.0,
     'L2_ffn_moe_b1': 21.639,
     'L2_ffn_moe_b2': 4.413,
     'L3_gnn_a_sa': 3.667,
     'L3_gnn_b_gcnb': 8.0,
     'L3_gnn_Wa': 4.741,
     'L3_gnn_Wb': 4.164}
    for name, (base, spread) in spreads.items():
        noise = np.random.default_rng([zlib.crc32(name.encode()), seed]).standard_normal(out[name].shape)
        drawn = base * np.exp(spread * noise) if base else spread * noise
        out[name] = jnp.asarray(drawn.astype(out[name].dtype))
    for name, factor in factors.items():
        out[name] = (out[name] * factor).astype(out[name].dtype)
    return out
```

```python
from contextlib import ExitStack

import concourse.bass as bass
from concourse import mybir

F32 = mybir.dt.float32
F16 = mybir.dt.float16
ALU = mybir.AluOpType
ACT = mybir.ActivationFunctionType
AX_X = mybir.AxisListType.X

P = 128
N = 1354
D = 256
KD = D // P
NT = -(-N // P)
LAST = N - (NT - 1) * P
CW = 512
NC = -(-N // CW)
TPC = CW // P
XC = D + 4
DI = 512
DB = DI // P
DS = 16
DR = 16
TAPS = 4
MW = 452
MN = NC * MW
EPS = 1e-5
NEG = -10000000000.0
H_BANKS, Y_BANKS = 4, 2

CHUNK_W = [min(CW, N - c * CW) for c in range(NC)]
CHUNK_T = [range(c * TPC, min((c + 1) * TPC, NT)) for c in range(NC)]


def rows(t):
    return P if t < NT - 1 else LAST


FFN = {"f0": (8, 4), "f1": (10, 8), "f2": (2, 4), "f3": (8, 8)}
T_ITEMS = KD * NC
STAGES = [
    ("g0", T_ITEMS + NC, 2 * NT),
    ("t_f0", T_ITEMS, 0),
    ("f0", 8 * NC * 4, 8 * NT),
    ("g1", 0, NT),
    ("t_f1", T_ITEMS, 0),
    ("f1", 10 * NC * 8, 10 * NT),
    ("g2", 2 * T_ITEMS, 2 * NT),
    ("mamba_in", T_ITEMS + DB * NC + NC, 0),
    ("mamba_scan", NC * 2 * DB, 0),
    ("mamba_out", 0, NT),
    ("t_f2", T_ITEMS, 0),
    ("f2", 2 * NC * 4, 2 * NT),
    ("g3", T_ITEMS + NC, 4 * NT),
    ("t_f3", T_ITEMS, 0),
    ("f3", 8 * NC * 8, 8 * NT),
]
H0, Y0 = {}, {}
_h = _y = 0
for _name, _nh, _ny in STAGES:
    H0[_name], Y0[_name] = _h, _y
    _h, _y = _h + _nh, _y + _ny
Y_END = _y
LOADS0 = {"f0": 0, "f1": 8, "f2": 18, "f3": 20}
XS, WS, HS = 256.0, 256.0, 64.0
PIECE = 1024
PIECES = {k: 2 * fb * KD * P // PIECE for k, (_, fb) in FFN.items()}
PIECE0, ITEM0 = {}, {}
_p = _i = 0
for _name, (_e, _fb) in FFN.items():
    PIECE0[_name], ITEM0[_name] = _p, _i
    _p, _i = _p + _e * PIECES[_name], _i + _e * NC * _fb
X_SPLIT0 = {"f0": 0, "f1": 1, "f2": 2, "f3": 3}
LN = {n: i for i, n in enumerate(["g0", "f0", "g1", "f1", "g2", "m_a", "m_b", "f2", "g3", "f3"])}
GATE = {"f0": 0, "f1": 1, "f3": 2}
DMA = 16


def build(nc, a, out):
    ctx = ExitStack()
    with ctx:
        def sb(name, shape):
            return ctx.enter_context(nc.sbuf_tensor(name, shape, F32))

        def sb16(name, shape):
            return ctx.enter_context(nc.sbuf_tensor(name, shape, F16))

        def sem(name):
            return ctx.enter_context(nc.semaphore(name))

        x = sb("x", [P, NT, D])
        xn = sb("xn", [P, NT, XC])
        xT = sb("xT", [P, KD * NT * P])
        adjT = sb("adjT", [P, NT * N])
        wparts = sb16("wparts", [P, 2, 2, 2, 8 * D])
        stage = sb("stage", [P, 2, PIECE])
        b1 = sb("b1", [P, 2, 8])
        b2 = sb("b2", [P, 2, D])
        work = sb("work", [P, 2 * NT * CW])
        V = sb("V", [P, NT * XC])
        row = sb("row", [P, MN])
        gw = sb("gw", [P, KD * D])
        ident = sb("ident", [P, P])
        ones = sb("ones", [P, P])
        before = sb("before", [P, 64])
        bias0 = sb("bias0", [P, D])
        bias3 = sb("bias3", [P, D])
        wgate = sb("wgate", [P, 3, KD, 8])
        bgate = sb("bgate", [P, 8])
        bnode = sb("bnode", [P, KD])
        bab = sb("bab", [P, 2])
        mcw = sb("mcw", [P, DB, TAPS])
        mcb = sb("mcb", [P, DB])
        mdb = sb("mdb", [P, DB])
        mds = sb("mds", [P, DB])
        malog = sb("malog", [P, DB * DS])
        mA = sb("mA", [P, DB * DS])
        carry = sb("carry", [P, DB * DS])
        dbcc = sb("dbcc", [48, MW])
        gates = sb("gates", [P, NT, 10])
        gates_s = sb("gates_s", [P, NT, 10])
        lg = sb("lg", [P, NT, 8])
        pr = sb("pr", [P, NT, 8])
        rank = sb("rank", [P, NT, 8])
        gmx = sb("gmx", [P, NT])
        gsum = sb("gsum", [P, NT])
        st = sb("st", [P, NT, 6])
        mv = sb("mv", [P, NT, 2])
        var = sb("var", [P, NT])
        std = sb("std", [P, NT])
        rstd = sb("rstd", [P, NT])
        deg = sb("deg", [P, NT])
        dsq = sb("dsq", [P, NT])
        dinv = sb("dinv", [P, NT])
        sig = sb("sig", [P, NT, 2])
        rc = sb("rc", [P, 2, 2])
        tmp = sb("tmp", [P, 2, D])

        xT3 = xT[:, :].rearrange("p (k n) -> p k n", k=KD)
        adj3 = adjT[:, :].rearrange("p (j n) -> p j n", j=NT)
        V3 = V[:, :].rearrange("p (j n) -> p j n", j=NT)
        block3 = [work[:, h * NT * CW:(h + 1) * NT * CW].rearrange("p (j n) -> p j n", j=NT) for h in range(2)]
        hT = {fb: [[work[:, h * fb * CW:(h + 1) * fb * CW].bitcast(F16)[:, q * fb * CW:(q + 1) * fb * CW]
                    .rearrange("p (f n) -> p f n", f=fb) for q in range(2)] for h in range(2)] for fb in (4, 8)}
        x16 = [work[:, 8192:8192 + KD * NT * P].bitcast(F16)[:, q * KD * NT * P:(q + 1) * KD * NT * P]
               .rearrange("p (k n) -> p k n", k=KD) for q in range(2)]
        hraw = xn[:, :, :].rearrange("p t n -> p (t n)")[:, 0:4 * CW].rearrange("p (r n) -> p r n", r=4)
        cnt = work[:, 4096:4096 + N]
        mxp = work[:, 4096 + N:4096 + 2 * N]
        rsum = work[:, 4096 + 2 * N:4096 + 3 * N]
        cmp = [V[:, N + 704 * i:N + 704 * (i + 1)] for i in range(2)]
        nB = V[:, 0:N]
        dscr = tmp[:, 0, 0:P]
        g0w = gw[:, 0:KD * D].rearrange("p (k n) -> p k n", k=KD)
        g2n = gw[:, 0:KD * D].rearrange("p (k n) -> p k n", k=KD)
        spare = block3[1].rearrange("p j n -> p (j n)")
        g2k = spare[:, 3072:3072 + 4 * KD * D].rearrange("p (h k n) -> p h k n", h=4, k=KD)
        g3r = spare[:, 0:KD * XC].rearrange("p (k n) -> p k n", k=KD)
        g3l = spare[:, 520:520 + KD * XC].rearrange("p (k n) -> p k n", k=KD)
        g3t = spare[:, 1040:1040 + KD * D].rearrange("p (k n) -> p k n", k=KD)
        g3a = spare[:, 1552:1552 + 4].rearrange("p (k n) -> p k n", k=KD)
        uT3 = spare[:, 0:3072].rearrange("p (k n) -> p k n", k=KD)
        xs = adjT[:, 0:DB * MN].rearrange("p (d n) -> p d n", d=DB)
        o = DB * MN
        delta, u, zg = [adjT[:, o + i * DB * MW:o + (i + 1) * DB * MW].rearrange("p (d n) -> p d n", d=DB)
                        for i in range(3)]
        o += 3 * DB * MW
        mwin = adjT[:, o:o + KD * 1024].rearrange("p (k n) -> p k n", k=KD)
        mwx = adjT[:, o + 2048:o + 2048 + DB * 48].rearrange("p (k n) -> p k n", k=DB)
        mwdt = adjT[0:DR, o + 2240:o + 2240 + DI]
        mwo = adjT[:, o + 2752:o + 2752 + DB * D].rearrange("p (k n) -> p k n", k=DB)
        xcp = [work[:, i * 1360:i * 1360 + TAPS - 1 + MN] for i in range(2)]
        cacc = [work[:, (2 + i) * 1360:(2 + i) * 1360 + MN] for i in range(2)]
        q = DB * MW
        dA = [work[:, i * q:(i + 1) * q].rearrange("p (d n) -> p d n", d=DB) for i in range(2)]
        hC = [work[:, (2 + i) * q:(3 + i) * q].rearrange("p (d n) -> p d n", d=DB) for i in range(2)]
        dBx = work[:, 4 * q:5 * q].rearrange("p (d n) -> p d n", d=DB)
        hS = work[:, 5 * q:6 * q].rearrange("p (d n) -> p d n", d=DB)
        dbc = row[0:48, 0:MN]
        xh = V[:, 0:NT * D].rearrange("p (j n) -> p j n", j=NT)
        XB = xT[:, 0:NT * D].rearrange("p (j n) -> p j n", j=NT)

        psH = [ctx.enter_context(nc.psum_tensor(f"psH{i}", [P, 512], F32)) for i in range(H_BANKS)]
        psY = [ctx.enter_context(nc.psum_tensor(f"psY{i}", [P, 512], F32)) for i in range(Y_BANKS)]
        psM = [ctx.enter_context(nc.psum_tensor(f"psM{i}", [P, 512], F32)) for i in range(2)]
        psB, psC = psY, psM

        x_in = sem("x_in")
        adj_in = [sem(f"adj_in{j}") for j in range(NT)]
        const_in = sem("const_in")
        gw_in = sem("gw_in")
        gk_in = sem("gk_in")
        mw_in = sem("mw_in")
        adj_again = sem("adj_again")
        b_in = [sem(f"b_in{s}") for s in range(2)]
        st_in = [sem(f"st_in{s}") for s in range(2)]
        w_hi = sem("w_hi")
        w_split = sem("w_split")
        x_hi = sem("x_hi")
        x_split = sem("x_split")
        h_hi = sem("h_hi")
        h_split = sem("h_split")
        h_done = sem("h_done")
        h_used = sem("h_used")
        y_done = sem("y_done")
        y_used = sem("y_used")
        chain = sem("chain")
        ln_var = sem("ln_var")
        ln_std = sem("ln_std")
        ln_out = sem("ln_out")
        g_done = sem("g_done")
        g_shift = sem("g_shift")
        g_exp = sem("g_exp")
        b_added = sem("b_added")
        part_done = sem("part_done")
        all_done = sem("all_done")
        cnt_root = sem("cnt_root")
        deg_max = sem("deg_max")
        deg_root = sem("deg_root")
        v_ready = sem("v_ready")
        blk_raw = sem("blk_raw")
        blk_exp = sem("blk_exp")
        blk = sem("blk")
        kmean = sem("kmean")
        a_done = sem("a_done")
        a_used = sem("a_used")
        za_ready = sem("za_ready")
        za_sig = sem("za_sig")
        fin_ready = sem("fin_ready")
        fin_sig = sem("fin_sig")
        act_chain = sem("act_chain")
        pad_zero = sem("pad_zero")
        conv_done = sem("conv_done")
        xs_ready = sem("xs_ready")
        sp_ready = sem("sp_ready")
        m_dA = sem("m_dA")
        m_bc = sem("m_bc")
        m_hc = sem("m_hc")
        m_acc = sem("m_acc")
        m_dbc = sem("m_dbc")
        m_chain = sem("m_chain")
        m_y = sem("m_y")
        out_done = sem("out_done")

        block = ctx.enter_context(nc.Block())

        @block.sync
        def _(sp):
            sp.dma_start(x[:, :, :], a["x"]).then_inc(x_in, DMA)
            for j in range(NT):
                sp.dma_start(adj3[:, j, :], a["adj"][:, j, :]).then_inc(adj_in[j], DMA)

            def load_expert(stage_, e, slot, q):
                k, n = stage_[1], PIECES[stage_]
                fb = FFN[stage_][1]
                sp.dma_start(b1[:, slot, 0:fb], a[f"b1_{k}"][bass.ds(e, 1)].rearrange("a p f -> (a p) f")).then_inc(b_in[slot], DMA)
                sp.dma_start(b2[:, slot, :], a[f"b2_{k}"][bass.ds(e, 1)].broadcast_to([P, D])).then_inc(b_in[slot], DMA)
                for i in range(n):
                    w = a[f"w{1 + i // (n // 2)}_{k}"][bass.ds(e, 1)].rearrange("a p f -> (a p) f")
                    o_ = i % (n // 2) * PIECE
                    sp.wait_ge(w_split, q + (i + 1))
                    sp.dma_start(stage[:, i % 2, :], w[:, o_:o_ + PIECE]).then_inc(st_in[i % 2], DMA)

            def load_first(stage_, before_stage):
                for s in range(2):
                    if before_stage:
                        n = FFN[before_stage][0]
                        sp.wait_ge(y_used, Y_BANKS + Y0[before_stage] + NT * (n - 1 + s))
                    load_expert(stage_, s, s, PIECE0[stage_] + s * PIECES[stage_])

            def load_rest(stage_):
                n = FFN[stage_][0]
                with sp.Fori(1, n // 2) as pair:
                    for s in range(2):
                        sp.wait_ge(y_used, pair * 2 * NT + (Y_BANKS + Y0[stage_] + NT * (s - 1)))
                        load_expert(stage_, pair * 2 + s, s, pair * (2 * PIECES[stage_]) + (PIECE0[stage_] + s * PIECES[stage_]))

            load_first("f0", None)
            load_rest("f0")
            load_first("f1", "f0")
            load_rest("f1")
            load_first("f2", "f1")
            load_first("f3", "f2")
            load_rest("f3")
            sp.wait_ge(y_used, Y_BANKS + Y_END)
            sp.dma_start(out[0:(NT - 1) * P, :].rearrange("(t p) d -> p t d", p=P), x[:, 0:NT - 1, :]).then_inc(out_done, DMA)
            sp.dma_start(out[(NT - 1) * P:N, :], x[0:LAST, NT - 1, :]).then_inc(out_done, DMA)
            sp.wait_ge(out_done, 2 * DMA)

        @block.gpsimd
        def _(pool):
            n_const = 0
            for dst, key in ((ident[:, :], "ident"), (ones[:, :], "ones"), (before[:, :], "before"), (wgate[:, :, :, :], "wgate"),
                             (bnode[:, :], "bnode"), (mcw[:, :, :], "mcw"), (mcb[:, :], "mcb"), (mdb[:, :], "mdb"),
                             (mds[:, :], "mds"), (malog[:, :], "malog")):
                pool.dma_start(dst, a[key]).then_inc(const_in, DMA)
                n_const += 1
            for dst, key, w in ((bias0[:, :], "bias0", D), (bias3[:, :], "bias3", D), (bgate[:, :], "bgate", 8), (bab[:, :], "bab", 2)):
                pool.dma_start(dst, a[key].broadcast_to([P, w])).then_inc(const_in, DMA)
                n_const += 1
            assert n_const == N_CONST
            pool.dma_start(g0w, a["g0w"]).then_inc(gw_in, DMA)
            pool.wait_ge(part_done, 1)
            pool.wait_ge(y_used, Y_BANKS + Y0["f0"])
            pool.partition_all_reduce(nB, cnt, P, bass.bass_isa.ReduceOp.add).then_inc(all_done, 1)
            pool.partition_all_reduce(row[:, 0:N], mxp, P, bass.bass_isa.ReduceOp.max).then_inc(all_done, 1)
            pool.dma_start(g2n, a["g2n"]).then_inc(gw_in, DMA)
            pool.wait_ge(y_used, Y_BANKS + Y0["g2"])
            pool.dma_start(g2k, a["g2k"]).then_inc(gk_in, DMA)
            pool.wait_ge(blk_exp, NC)
            for dst, key in ((mwin, "mwin"), (mwx, "mwx"), (mwdt, "mwdt"), (mwo, "mwo")):
                pool.dma_start(dst, a[key]).then_inc(mw_in, DMA)
            pool.wait_ge(y_used, Y_BANKS + Y0["f2"])
            pool.dma_start(adjT[:, :], a["adj"].rearrange("p j n -> p (j n)")).then_inc(adj_again, DMA)
            pool.wait_ge(y_used, Y_BANKS + Y0["g3"])
            for dst, key in ((g3t, "g3t"), (g3a, "g3a"), (g3l[:, :, 0:D + 2], "g3l"), (g3r[:, :, 0:D], "g3sa"),
                             (g3r[:, :, D + 2:D + 4], "g3x")):
                pool.dma_start(dst, a[key]).then_inc(gw_in, DMA)
            pool.wait_ge(adj_again, DMA)

        @block.tensor
        def _(pe):
            pe.sem_inc(y_done, 1)
            pe.wait_ge(const_in, DMA * N_CONST)

            def transposes(src, stage, ln):
                pe.wait_ge(ln_out, LN[ln] + 1)
                i = H0[stage]
                for k in range(KD):
                    for c in range(NC):
                        pe.wait_ge(h_used, i + 1)
                        for n, t in enumerate(CHUNK_T[c]):
                            last = nc.tensor.transpose(psH[i % H_BANKS][:, n * P:(n + 1) * P],
                                                       src[:, t, k * P:(k + 1) * P], ident[:, :])
                        last.then_inc(h_done, 1)
                        i += 1
                pe.wait_ge(h_used, H_BANKS + i)

            def gate_logits(stage):
                g = GATE[stage]
                for t in range(NT):
                    for k in range(KD):
                        last = nc.tensor.matmul(psM[0][:, t * 8:(t + 1) * 8], xT3[:, k, t * P:(t + 1) * P],
                                                wgate[:, g, k, :], start=(k == 0), stop=(k == KD - 1))
                last.then_inc(g_done, 1)

            def ffn(stage):
                experts, fb = FFN[stage]
                h0, y0, i0 = H0[stage], Y0[stage], ITEM0[stage]
                per_h, per_y, per_w = 2 * NC * fb, 2 * NT, 2 * PIECES[stage]
                parts = ((0, 0), (0, 1), (1, 0))
                pe.wait_ge(x_split, X_SPLIT0[stage] + 1)

                def body(pair):
                    def hidden(s, c):
                        for f in range(fb):
                            i = (s * NC + c) * fb + f
                            pe.wait_ge(h_used, pair * per_h + (h0 + i + 1))
                            for k in range(KD):
                                for wq, xq in parts:
                                    last = nc.tensor.matmul(psH[(h0 + i) % H_BANKS][:, 0:CHUNK_W[c]],
                                                            wparts[:, s, 0, wq, (k * fb + f) * P:(k * fb + f + 1) * P],
                                                            x16[xq][:, k, c * CW:c * CW + CHUNK_W[c]],
                                                            start=(k == wq == xq == 0), stop=(k == KD - 1 and wq == 1))
                            last.then_inc(h_done, 1)

                    def output(s, c):
                        pe.wait_ge(h_split, pair * (per_h // 2) + (2 + (i0 + (s * NC + c + 1) * fb) // 2))
                        for n, t in enumerate(CHUNK_T[c]):
                            i = s * NT + t
                            pe.wait_ge(y_used, pair * per_y + (y0 + i + 1))
                            for f in range(fb):
                                for hq, wq in parts:
                                    last = nc.tensor.matmul(psY[(y0 + i) % Y_BANKS][0:rows(t), 0:D],
                                                            hT[fb][(s * NC + c) % 2][hq][:, f, n * P:n * P + rows(t)],
                                                            wparts[:, s, 1, wq, f * D:(f + 1) * D],
                                                            start=(f == hq == wq == 0), stop=(f == fb - 1 and hq == 1))
                            last.then_inc(y_done, 1)

                    order = [(s, c) for s in range(2) for c in range(NC)]
                    for n, (s, c) in enumerate(order):
                        if c == 0:
                            pe.wait_ge(w_split, pair * per_w + (2 + PIECE0[stage] + (s + 1) * PIECES[stage]))
                        hidden(s, c)
                        if n:
                            output(*order[n - 1])
                    output(*order[-1])

                if experts > 2:
                    with pe.Fori(0, experts // 2 - 1) as pair:
                        body(pair)
                body(experts // 2 - 1)

            def attend(y, tiles, src, off, values, cols):
                for t in tiles:
                    pe.wait_ge(y_used, y + 1)
                    for j in range(NT):
                        last = nc.tensor.matmul(psY[y % Y_BANKS][0:rows(t), 0:cols],
                                                src[0:rows(j), j, t * P - off:t * P - off + rows(t)],
                                                values[0:rows(j), j, 0:cols], start=(j == 0), stop=(j == NT - 1))
                    last.then_inc(y_done, 1)
                    y += 1
                return y

            def project(y, src3, w3, blocks, cols):
                for t in range(NT):
                    pe.wait_ge(y_used, y + 1)
                    for k in range(blocks):
                        last = nc.tensor.matmul(psY[y % Y_BANKS][0:rows(t), 0:cols], src3[:, k, t * P:t * P + rows(t)],
                                                w3[:, k, 0:cols], start=(k == 0), stop=(k == blocks - 1))
                    last.then_inc(y_done, 1)
                    y += 1
                return y

            transposes(xn, "g0", "g0")
            i = H0["g0"] + T_ITEMS
            for c in range(NC):
                pe.wait_ge(h_used, i + 1)
                for j in range(NT):
                    pe.wait_ge(adj_in[j], DMA)
                    last = nc.tensor.matmul(psH[i % H_BANKS][:, 0:CHUNK_W[c]], ones[:, :],
                                            adj3[:, j, c * CW:c * CW + CHUNK_W[c]], start=(j == 0), stop=(j == NT - 1))
                last.then_inc(h_done, 1)
                i += 1
            pe.wait_ge(gw_in, DMA)
            y = project(Y0["g0"], xT3, g0w, KD, D)
            pe.wait_ge(v_ready, 1)
            attend(y, range(NT), adj3, 0, V3, D)
            transposes(xn, "t_f0", "f0")
            gate_logits("f0")
            ffn("f0")
            pe.wait_ge(ln_out, LN["g1"] + 1)
            y = Y0["g1"]
            for c in range(NC):
                pe.wait_ge(blk, c + 1)
                y = attend(y, CHUNK_T[c], block3[c % 2], c * CW, xn, D + 1)
            transposes(xn, "t_f1", "f1")
            gate_logits("f1")
            ffn("f1")
            transposes(xn, "g2", "g2")
            pe.wait_ge(gw_in, 2 * DMA)
            i = H0["g2"] + T_ITEMS
            for k2 in range(KD):
                for c in range(NC):
                    pe.wait_ge(h_used, i + 1)
                    for k in range(KD):
                        last = nc.tensor.matmul(psH[i % H_BANKS][:, 0:CHUNK_W[c]], g2n[:, k, k2 * P:(k2 + 1) * P],
                                                xT3[:, k, c * CW:c * CW + CHUNK_W[c]], start=(k == 0), stop=(k == KD - 1))
                    last.then_inc(h_done, 1)
                    i += 1
            pe.wait_ge(h_used, H_BANKS + i)
            pe.wait_ge(kmean, 1)
            y = project(Y0["g2"], uT3, g2k[:, 0], KD, D)
            pe.wait_ge(v_ready, 2)
            for c in range(NC):
                pe.wait_ge(blk_exp, c + 1)
                y = attend(y, CHUNK_T[c], block3[c % 2], c * CW, V3, D + 1)
            transposes(xh, "mamba_in", "m_b")
            pe.wait_ge(mw_in, 4 * DMA)
            i = H0["mamba_in"] + T_ITEMS
            for d in range(DB):
                for c in range(NC):
                    pe.wait_ge(h_used, i + 1)
                    for k in range(KD):
                        last = nc.tensor.matmul(psH[i % H_BANKS][:, 0:MW], mwin[:, k, d * P:(d + 1) * P],
                                                xT3[:, k, c * MW:(c + 1) * MW], start=(k == 0), stop=(k == KD - 1))
                    last.then_inc(h_done, 1)
                    i += 1
            pe.wait_ge(xs_ready, DB)
            for c in range(NC):
                pe.wait_ge(h_used, i + 1)
                for k in range(DB):
                    last = nc.tensor.matmul(psH[i % H_BANKS][0:48, 0:MW], mwx[:, k, :], xs[:, k, c * MW:(c + 1) * MW],
                                            start=(k == 0), stop=(k == DB - 1))
                last.then_inc(h_done, 1)
                i += 1
            pe.wait_ge(h_used, H_BANKS + i)
            with pe.Fori(0, NC) as c:
                i = H0["mamba_scan"]
                for d in range(DB):
                    pe.wait_ge(h_used, c * (2 * DB) + (i + 1))
                    if d == 0:
                        pe.wait_ge(m_y, c + 1)
                        pe.wait_ge(m_dbc, c + 1)
                    nc.tensor.matmul(psH[i % H_BANKS][:, 0:MW], mwdt[:, d * P:(d + 1) * P], dbcc[0:DR, :],
                                     start=True, stop=True).then_inc(h_done, 1)
                    i += 1
                for d in range(DB):
                    pe.wait_ge(h_used, c * (2 * DB) + (i + 1))
                    for k in range(KD):
                        last = nc.tensor.matmul(psH[i % H_BANKS][:, 0:MW], mwin[:, k, DI + d * P:DI + (d + 1) * P],
                                                xT3[:, k, bass.ds(c * MW, MW)], start=(k == 0), stop=(k == KD - 1))
                    last.then_inc(h_done, 1)
                    i += 1
                pe.wait_ge(h_used, c * (2 * DB) + (H_BANKS + i))

                def spread(n):
                    pe.wait_ge(m_hc, c * DS + (n + 1))
                    nc.tensor.matmul(psB[n % 2][:, 0:MW], ident[0:48, DR + n:DR + n + 1].broadcast_to([48, P]),
                                     dbcc[:, :], start=True, stop=True)
                    nc.tensor.matmul(psC[n % 2][:, 0:MW], ident[0:48, DR + DS + n:DR + DS + n + 1].broadcast_to([48, P]),
                                     dbcc[:, :], start=True, stop=True).then_inc(m_bc, 1)

                spread(0)
                spread(1)
                for n in range(DS):
                    pe.wait_ge(m_hc, c * DS + (n + 3))
                    for d in range(DB):
                        last = nc.tensor.matmul(psH[(H0["mamba_scan"] + d) % H_BANKS][:, 0:MW], ident[:, :], hC[n % 2][:, d, :],
                                                start=(n == 0), stop=(n == DS - 1))
                    last.then_inc(m_acc, 1)
                    if n + 2 < DS:
                        spread(n + 2)
            pe.wait_ge(m_y, NC + 1)
            project(Y0["mamba_out"], xs, mwo, DB, D)
            transposes(xh, "t_f2", "f2")
            ffn("f2")
            transposes(xn, "g3", "g3")
            pe.wait_ge(gw_in, 7 * DMA)
            for k2 in range(KD):
                for k in range(KD):
                    last = nc.tensor.matmul(psM[0][:, 2 * k2:2 * k2 + 2], g3t[:, k, k2 * P:(k2 + 1) * P], g3a[:, k, :],
                                            start=(k == 0), stop=(k == KD - 1))
            last.then_inc(a_done, 1)
            y = project(Y0["g3"], xT3, g3l, KD, D + 2)
            pe.wait_ge(a_used, 1)
            i = H0["g3"] + T_ITEMS
            for c in range(NC):
                pe.wait_ge(h_used, i + 1)
                for k in range(KD):
                    last = nc.tensor.matmul(psH[i % H_BANKS][:, 0:CHUNK_W[c]], g3r[:, k, D:D + 1].broadcast_to([P, P]),
                                            xT3[:, k, c * CW:c * CW + CHUNK_W[c]], start=(k == 0), stop=(k == KD - 1))
                last.then_inc(h_done, 1)
                i += 1
            y = project(y, xT3, g3r, KD, XC)
            pe.wait_ge(v_ready, 3)
            pe.wait_ge(adj_again, DMA)
            y = attend(y, range(NT), adj3, 0, V3, D + 2)
            for c in range(NC):
                pe.wait_ge(blk, NC + c + 1)
                y = attend(y, CHUNK_T[c], block3[c % 2], c * CW, xn, D + 1)
            transposes(xn, "t_f3", "f3")
            gate_logits("f3")
            ffn("f3")

        @block.scalar
        def _(act):
            act.sem_inc(h_used, H_BANKS)
            n_own = [0]

            def own(ins):
                n_own[0] += 1
                ins.then_inc(act_chain, 1)
                act.wait_ge(act_chain, n_own[0])

            def ln_root(ln):
                act.wait_ge(ln_var, LN[ln] + 1)
                nc.scalar.activation(std[:, :], var[:, :], ACT.Sqrt).then_inc(ln_std, 1)

            def take(i, dst, width, func=ACT.Copy, rows_=P, **kw):
                act.wait_ge(h_done, i + 1)
                nc.scalar.activation(dst, psH[i % H_BANKS][0:rows_, 0:width], func, **kw).then_inc(h_used, 1)

            def take_transposes(stage, split=False):
                i = H0[stage]
                for k in range(KD):
                    for c in range(NC):
                        w = len(CHUNK_T[c]) * P
                        if split:
                            act.wait_ge(h_done, i + 1)
                            last = nc.scalar.activation(x16[0][:, k, c * CW:c * CW + w], psH[i % H_BANKS][:, 0:w], ACT.Copy, scale=XS)
                            last.then_inc(x_hi, 1)
                        take(i, xT3[:, k, c * CW:c * CW + w], w)
                        i += 1

            def weights_hi(stage_, pair, e, i):
                n = PIECES[stage_]
                q = PIECE0[stage_] + e * n + i
                act.wait_ge(st_in[i % 2], pair * (n * DMA) + (q // 2 + 1) * DMA)
                dst = wparts[:, e % 2, i // (n // 2), 0, i % (n // 2) * PIECE:(i % (n // 2) + 1) * PIECE]
                nc.scalar.activation(dst, stage[:, i % 2, :], ACT.Copy, scale=WS).then_inc(w_hi, 1)

            def first_weights_hi(stage_, half):
                for i in range(2 * half, min(2 * half + 2, PIECES[stage_])):
                    weights_hi(stage_, 0, 0, i)

            def gate_exp(stage, scale):
                act.wait_ge(g_shift, GATE[stage] + 1)
                nc.scalar.activation(pr[:, :, :], lg[:, :, :], ACT.Exp, scale=scale).then_inc(g_exp, 1)

            def ffn(stage_, func):
                experts, fb = FFN[stage_]
                h0, i0 = H0[stage_], ITEM0[stage_]

                def body(pair, last_pair):
                    for s in range(2):
                        act.wait_ge(b_in[s], pair * (2 * DMA) + 2 * DMA * (LOADS0[stage_] // 2 + 1))
                        for c in range(NC):
                            for f in range(fb):
                                i = (s * NC + c) * fb + f
                                if f % 2 == 0:
                                    act.wait_ge(h_split, pair * (NC * fb) + ((i0 + i) // 2 + 1))
                                act.wait_ge(h_done, pair * (2 * NC * fb) + (h0 + i + 1))
                                nc.scalar.activation(hraw[:, (i0 + i) % 4, 0:CHUNK_W[c]], psH[(h0 + i) % H_BANKS][:, 0:CHUNK_W[c]],
                                                     func, bias=b1[:, s, f:f + 1], scale=1.0 / (XS * WS)).then_inc(h_used, 1)
                            if c == 1 and not (s == 1 and last_pair):
                                for i in range(PIECES[stage_]):
                                    weights_hi(stage_, pair, s + 1, i)

                if experts > 2:
                    with act.Fori(0, experts // 2 - 1) as pair:
                        body(pair, False)
                body(experts // 2 - 1, True)

            ln_root("g0")
            take_transposes("g0")
            for c in range(NC):
                take(H0["g0"] + T_ITEMS + c, rsum[:, c * CW:c * CW + CHUNK_W[c]], CHUNK_W[c])
            first_weights_hi("f0", 0)
            act.wait_ge(deg_max, 1)
            nc.scalar.activation(dsq[:, :], dinv[:, :], ACT.Sqrt).then_inc(deg_root, 1)
            ln_root("f0")
            first_weights_hi("f0", 1)
            take_transposes("t_f0", split=True)
            gate_exp("f0", 1.0)
            ffn("f0", ACT.Gelu_apprx_tanh)
            act.wait_ge(all_done, 1)
            nc.scalar.activation(nB, nB, ACT.Sqrt).then_inc(cnt_root, 1)
            ln_root("g1")
            first_weights_hi("f1", 0)
            ln_root("f1")
            first_weights_hi("f1", 1)
            take_transposes("t_f1", split=True)
            gate_exp("f1", 1.0)
            ffn("f1", ACT.Gelu)
            ln_root("g2")
            take_transposes("g2")
            i = H0["g2"] + T_ITEMS
            for k2 in range(KD):
                for c in range(NC):
                    take(i, uT3[:, k2, c * CW:c * CW + CHUNK_W[c]], CHUNK_W[c], ACT.Identity, bias=bnode[:, k2:k2 + 1])
                    i += 1
            for c in range(NC):
                act.wait_ge(blk_raw, c + 1)
                b = block3[c % 2][:, :, 0:CHUNK_W[c]]
                nc.scalar.activation(b, b, ACT.Exp).then_inc(blk_exp, 1)
            ln_root("m_a")
            ln_root("m_b")
            take_transposes("mamba_in")
            i = H0["mamba_in"] + T_ITEMS
            own(nc.scalar.activation(mA[:, :], malog[:, :], ACT.Exp))
            own(nc.scalar.activation(mA[:, :], mA[:, :], ACT.Copy, scale=-1.0))

            def silu_of(d):
                act.wait_ge(conv_done, d + 1)
                nc.scalar.activation(xs[:, d, :], cacc[d % 2], ACT.Silu, bias=mcb[:, d:d + 1]).then_inc(xs_ready, 1)

            act.wait_ge(pad_zero, 1)
            for d in range(DB):
                if d >= 2:
                    silu_of(d - 2)
                for c in range(NC):
                    take(i, xcp[d % 2][:, TAPS - 1 + c * MW:TAPS - 1 + (c + 1) * MW], MW)
                    i += 1
            silu_of(DB - 2)
            silu_of(DB - 1)
            for c in range(NC):
                take(i, dbc[:, c * MW:(c + 1) * MW], MW, rows_=48)
                i += 1
            act.wait_ge(h_used, H_BANKS + i)
            mA3 = mA[:, :].rearrange("p (n d) -> p n d", d=DB)
            PER = 4
            with act.Fori(0, NC) as c:
                i = H0["mamba_scan"]
                act.wait_ge(m_y, c + 1)
                nc.scalar.activation(dbcc[:, :], dbc[:, bass.ds(c * MW, MW)], ACT.Copy).then_inc(m_dbc, 1)
                for d in range(DB):
                    act.wait_ge(h_done, c * (2 * DB) + (i + d + 1))
                    nc.scalar.activation(delta[:, d, :], psH[(i + d) % H_BANKS][:, 0:MW], ACT.Abs, bias=mdb[:, d:d + 1])\
                        .then_inc(act_chain, 1)
                    nc.scalar.activation(u[:, d, :], psH[(i + d) % H_BANKS][:, 0:MW], ACT.Relu, bias=mdb[:, d:d + 1])\
                        .then_inc(h_used, 1)
                act.wait_ge(act_chain, c * DB + (n_own[0] + DB))
                nc.scalar.activation(delta[:, :, :], delta[:, :, :], ACT.Exp, scale=-1.0).then_inc(sp_ready, 1)
                for d in range(DB):
                    act.wait_ge(h_done, c * (2 * DB) + (i + DB + d + 1))
                    nc.scalar.activation(zg[:, d, :], psH[(i + DB + d) % H_BANKS][:, 0:MW], ACT.Silu).then_inc(h_used, 1)
                act.wait_ge(m_chain, c * M_CHAIN + (len(LOG1P) + 1))
                for n in range(DS):
                    act.wait_ge(m_hc, c * DS + (n + 1))
                    for d in range(DB):
                        last = nc.scalar.activation(dA[n % 2][:, d, :], delta[:, d, :], ACT.Exp, scale=mA3[:, n, d:d + 1])
                    last.then_inc(m_dA, 1)
            n_own[0] += NC * DB
            first_weights_hi("f2", 0)
            ln_root("f2")
            first_weights_hi("f2", 1)
            take_transposes("t_f2", split=True)
            ffn("f2", ACT.Relu)
            ln_root("g3")
            take_transposes("g3")
            for c in range(NC):
                take(H0["g3"] + T_ITEMS + c, row[:, c * CW:c * CW + CHUNK_W[c]], CHUNK_W[c])
            for c in range(NC):
                act.wait_ge(blk_raw, NC + c + 1)
                b = block3[c % 2][:, :, 0:CHUNK_W[c]]
                nc.scalar.activation(b, b, ACT.Exp, scale=-1.0).then_inc(blk_exp, 1)
                if c == 1:
                    act.wait_ge(za_ready, 1)
                    nc.scalar.activation(sig[:, :, :], sig[:, :, :], ACT.Sigmoid).then_inc(za_sig, 1)
            first_weights_hi("f3", 0)
            act.wait_ge(fin_ready, 1)
            nc.scalar.activation(XB[:, 0:NT - 1, :], XB[:, 0:NT - 1, :], ACT.Sigmoid)
            nc.scalar.activation(XB[0:LAST, NT - 1, :], XB[0:LAST, NT - 1, :], ACT.Sigmoid).then_inc(fin_sig, 1)
            ln_root("f3")
            first_weights_hi("f3", 1)
            take_transposes("t_f3", split=True)
            gate_exp("f3", 1.0 / 2.5)
            ffn("f3", ACT.Gelu_apprx_tanh)

        @block.vector
        def _(dve):
            dve.sem_inc(y_used, Y_BANKS)
            dve.sem_inc(w_split, 2)
            dve.sem_inc(h_split, 2)
            dve.sem_inc(m_y, 1)
            dve.sem_inc(m_hc, 2)
            n_own = [0]
            tt, ts, stt = nc.vector.tensor_tensor, nc.vector.tensor_scalar, nc.vector.scalar_tensor_tensor

            def own(ins):
                n_own[0] += 1
                ins.then_inc(chain, 1)
                dve.wait_ge(chain, n_own[0])

            def layernorm(src, dst, ln):
                for t in range(NT):
                    last = nc.vector.bn_stats(st[:, t, :], src[:, t, 0:D])
                own(last)
                for t in range(NT):
                    last = nc.vector.bn_aggr(mv[:, t, :], st[:, t, :])
                own(last)
                ts(var[:, :], mv[:, :, 1], EPS, None, ALU.add).then_inc(ln_var, 1)
                dve.wait_ge(ln_std, LN[ln] + 1)
                own(nc.vector.reciprocal(rstd[:, :], std[:, :]))
                for t in range(NT):
                    last = ts(dst[:, t, 0:D], src[:, t, 0:D], mv[:, t, 0:1], rstd[:, t:t + 1], ALU.subtract, ALU.mult)
                last.then_inc(ln_out, 1)
                dve.wait_ge(ln_out, LN[ln] + 1)

            def weights_lo(stage_, pair, e, i):
                n = PIECES[stage_]
                dve.wait_ge(w_hi, pair * (2 * n) + (PIECE0[stage_] + e * n + i + 1))
                hi, lo = (wparts[:, e % 2, i // (n // 2), q, i % (n // 2) * PIECE:(i % (n // 2) + 1) * PIECE] for q in range(2))
                stt(lo, stage[:, i % 2, :], WS, hi, ALU.mult, ALU.subtract).then_inc(w_split, 1)

            def first_weights_lo(stage_, half):
                for i in range(2 * half, min(2 * half + 2, PIECES[stage_])):
                    weights_lo(stage_, 0, 0, i)

            def split_x(stage_):
                dve.wait_ge(x_hi, T_ITEMS * (X_SPLIT0[stage_] + 1))
                dve.wait_ge(h_used, H_BANKS + H0["t_" + stage_] + T_ITEMS)
                stt(x16[1], xT3, XS, x16[0], ALU.mult, ALU.subtract).then_inc(x_split, 1)

            def all_taken(stage):
                dve.wait_ge(y_used, Y_BANKS + Y0[stage])

            def wide(ap, n, w):
                return ap.unsqueeze(1).broadcast_to([P, n, w])

            def gating(stage, biased, renorm):
                g = GATE[stage]
                dve.wait_ge(g_done, g + 1)
                logits = psM[0][:, 0:NT * 8].rearrange("p (t e) -> p t e", e=8)

                def per_token(v):
                    return v[:, :].unsqueeze(2).broadcast_to([P, NT, 8])

                if biased:
                    own(tt(lg[:, :, :], logits, wide(bgate[:, :], NT, 8), ALU.add))
                else:
                    own(nc.vector.tensor_copy(lg[:, :, :], logits))
                own(nc.vector.tensor_reduce(gmx[:, :], lg[:, :, :], AX_X, ALU.max))
                tt(lg[:, :, :], lg[:, :, :], per_token(gmx), ALU.subtract).then_inc(g_shift, 1)
                dve.wait_ge(g_exp, g + 1)
                own(nc.vector.tensor_reduce(gsum[:, :], pr[:, :, :], AX_X, ALU.add))
                own(nc.vector.reciprocal(gsum[:, :], gsum[:, :]))
                own(tt(pr[:, :, :], pr[:, :, :], per_token(gsum), ALU.mult))
                c0, c1 = (v.rearrange("p (t e f) -> p t e f", e=8, f=8) for v in cmp)
                pf = pr[:, :, :].unsqueeze(2).broadcast_to([P, NT, 8, 8])
                pe_ = pr[:, :, :].unsqueeze(3).broadcast_to([P, NT, 8, 8])
                tt(c0, pf, pe_, ALU.is_gt)
                own(tt(c1, pf, pe_, ALU.is_equal))
                c1f = cmp[1].rearrange("p (t e) -> p t e", e=64)
                own(tt(c1f, c1f, wide(before[:, :], NT, 64), ALU.mult))
                own(tt(cmp[0], cmp[0], cmp[1], ALU.add))
                own(nc.vector.tensor_reduce(rank[:, :, :], c0, AX_X, ALU.add))
                own(stt(gates[:, :, 0:8], rank[:, :, :], 2.0, pr[:, :, :], ALU.is_lt, ALU.mult))
                if renorm:
                    own(nc.vector.tensor_reduce(gsum[:, :], gates[:, :, 0:8], AX_X, ALU.add))
                    own(nc.vector.reciprocal(gsum[:, :], gsum[:, :]))
                    own(tt(gates[:, :, 0:8], gates[:, :, 0:8], per_token(gsum), ALU.mult))

            def ffn(stage_):
                experts, fb = FFN[stage_]
                y0, h0, i0 = Y0[stage_], H0[stage_], ITEM0[stage_]
                own(ts(gates_s[:, :, :], gates[:, :, :], 1.0 / (HS * WS), None, ALU.mult))

                def body(pair, last_pair):
                    def gate(g, s, t):
                        return g[0:rows(t), t, bass.ds(pair * 2 + s, 1)]

                    def split(s, c):
                        w = CHUNK_W[c]
                        for f in range(0, fb, 2):
                            i = (s * NC + c) * fb + f
                            raw = hraw[:, (i0 + i) % 4:(i0 + i) % 4 + 2, 0:w]
                            hi, lo = (hT[fb][(s * NC + c) % 2][q][:, f:f + 2, 0:w] for q in range(2))
                            dve.wait_ge(h_used, pair * (2 * NC * fb) + (H_BANKS + h0 + i + 2))
                            ts(hi, raw, HS, None, ALU.mult).then_inc(h_hi, 1)
                            dve.wait_ge(h_hi, pair * (NC * fb) + ((i0 + i) // 2 + 1))
                            stt(lo, raw, HS, hi, ALU.mult, ALU.subtract).then_inc(h_split, 1)

                    def add_bias(s):
                        dve.wait_ge(b_in[s], pair * (2 * DMA) + 2 * DMA * (LOADS0[stage_] // 2 + 1))
                        dve.wait_ge(y_used, pair * (2 * NT) + (Y_BANKS + y0 + s * NT))
                        for t in range(NT):
                            last = stt(x[0:rows(t), t, :], b2[0:rows(t), s, :], gate(gates, s, t), x[0:rows(t), t, :], ALU.mult, ALU.add)
                        last.then_inc(b_added, 1)
                        dve.wait_ge(b_added, pair * 2 + (LOADS0[stage_] + s + 1))

                    def add_output(s, c):
                        if c == 0:
                            add_bias(s)
                        for n, t in enumerate(CHUNK_T[c]):
                            i = y0 + s * NT + t
                            dve.wait_ge(y_done, pair * (2 * NT) + (i + 2))
                            stt(x[0:rows(t), t, :], psY[i % Y_BANKS][0:rows(t), 0:D], gate(gates_s, s, t), x[0:rows(t), t, :],
                                ALU.mult, ALU.add).then_inc(y_used, 1)
                            if c == 0 and n < PIECES[stage_] and not (s == 1 and last_pair):
                                weights_lo(stage_, pair, s + 1, n)

                    order = [(s, c) for s in range(2) for c in range(NC)]
                    for n, (s, c) in enumerate(order):
                        split(s, c)
                        if n:
                            add_output(*order[n - 1])
                    add_output(*order[-1])

                if experts > 2:
                    with dve.Fori(0, experts // 2 - 1) as pair:
                        body(pair, False)
                body(experts // 2 - 1, True)

            nc.vector.memset(gates[:, :, :], 1.0)
            own(nc.vector.memset(xn[:, :, D:XC], 1.0))
            dve.wait_ge(x_in, DMA)
            layernorm(x, xn, "g0")
            dve.wait_ge(const_in, DMA * N_CONST)
            dve.wait_ge(adj_in[0], DMA)
            ts(cnt, adj3[:, 0, :], 0.0, None, ALU.is_gt)
            own(nc.vector.tensor_copy(mxp, adj3[:, 0, :]))
            for j in range(1, NT):
                dve.wait_ge(adj_in[j], DMA)
                stt(cnt, adj3[:, j, :], 0.0, cnt, ALU.is_gt, ALU.add)
                own(tt(mxp[0:rows(j), :], mxp[0:rows(j), :], adj3[0:rows(j), j, :], ALU.max))
            dve.sem_inc(part_done, 1)
            first_weights_lo("f0", 0)
            own(nc.vector.memset(deg[:, :], 0.0))
            dve.wait_ge(h_used, H_BANKS + H0["g0"] + T_ITEMS + NC)
            for t in range(NT):
                r = rows(t)
                own(tt(dscr[0:r, 0:r], rsum[0:r, t * P:t * P + r], ident[0:r, 0:r], ALU.mult))
                own(nc.vector.tensor_reduce(deg[0:r, t:t + 1], dscr[0:r, 0:r], AX_X, ALU.add))
            ts(dinv[:, :], deg[:, :], 1e-35, None, ALU.max).then_inc(deg_max, 1)
            dve.wait_ge(deg_root, 1)
            own(nc.vector.reciprocal(dinv[:, :], dsq[:, :]))
            own(stt(dinv[:, :], deg[:, :], 0.0, dinv[:, :], ALU.is_gt, ALU.mult))
            y = Y0["g0"]
            for t in range(NT):
                dve.wait_ge(y_done, y + 2)
                ts(V3[0:rows(t), t, 0:D], psY[y % Y_BANKS][0:rows(t), 0:D], dinv[0:rows(t), t:t + 1], None, ALU.mult).then_inc(y_used, 1)
                y += 1
            dve.wait_ge(y_used, Y_BANKS + y)
            dve.sem_inc(v_ready, 1)
            for t in range(NT):
                r = rows(t)
                dve.wait_ge(y_done, y + 2)
                stt(tmp[0:r, t % 2, :], psY[y % Y_BANKS][0:r, 0:D], dinv[0:r, t:t + 1], bias0[0:r, :], ALU.mult, ALU.add).then_inc(y_used, 1)
                y += 1
                dve.wait_ge(y_used, Y_BANKS + y)
                last = stt(x[0:r, t, :], tmp[0:r, t % 2, :], 0.0, x[0:r, t, :], ALU.max, ALU.add)
            own(last)
            layernorm(x, xn, "f0")
            first_weights_lo("f0", 1)
            split_x("f0")
            gating("f0", False, False)
            ffn("f0")
            all_taken("g1")
            layernorm(x, xn, "g1")
            own(nc.vector.memset(xn[:, :, D:XC], 1.0))
            dve.wait_ge(all_done, 2)
            dve.wait_ge(cnt_root, 1)
            own(ts(nB, nB, 1e-12, None, ALU.max))
            own(nc.vector.reciprocal(nB, nB))

            def block1(c):
                b, w = block3[c % 2][:, :, 0:CHUNK_W[c]], CHUNK_W[c]
                av = adj3[:, :, c * CW:c * CW + w]
                own(stt(b, av, 0.0, wide(nB[:, c * CW:c * CW + w], NT, w), ALU.is_gt, ALU.mult))
                tt(b, b, av, ALU.add).then_inc(blk, 1)

            def take1(c):
                for t in CHUNK_T[c]:
                    r, y = rows(t), Y0["g1"] + t
                    dve.wait_ge(y_done, y + 2)
                    own(nc.vector.reciprocal(rc[0:r, 0, 0:1], psY[y % Y_BANKS][0:r, D:D + 1]))
                    stt(x[0:r, t, :], psY[y % Y_BANKS][0:r, 0:D], rc[0:r, 0, 0:1], x[0:r, t, :], ALU.mult, ALU.add).then_inc(y_used, 1)
                    dve.wait_ge(y_used, Y_BANKS + y + 1)

            block1(0)
            block1(1)
            take1(0)
            block1(2)
            take1(1)
            first_weights_lo("f1", 0)
            take1(2)
            layernorm(x, xn, "f1")
            first_weights_lo("f1", 1)
            split_x("f1")
            gating("f1", True, False)
            ffn("f1")
            all_taken("g2")
            layernorm(x, xn, "g2")
            dve.wait_ge(gk_in, DMA)
            own(tt(g2k[:, 0], g2k[:, 0], g2k[:, 1], ALU.add))
            own(tt(g2k[:, 0], g2k[:, 0], g2k[:, 2], ALU.add))
            own(tt(g2k[:, 0], g2k[:, 0], g2k[:, 3], ALU.add))
            ts(g2k[:, 0], g2k[:, 0], 0.25, None, ALU.mult).then_inc(kmean, 1)
            own(ts(row[:, 0:N], row[:, 0:N], -1.0, 1.0, ALU.mult, ALU.add))
            own(ts(row[:, 0:N], row[:, 0:N], NEG, None, ALU.mult))

            def block2(c):
                b, w = block3[c % 2][:, :, 0:CHUNK_W[c]], CHUNK_W[c]
                own(ts(b, adj3[:, :, c * CW:c * CW + w], -1.0, 1.0, ALU.mult, ALU.add))
                stt(b, b, NEG, wide(row[:, c * CW:c * CW + w], NT, w), ALU.mult, ALU.subtract).then_inc(blk_raw, 1)

            def take2(c):
                for t in CHUNK_T[c]:
                    r, y = rows(t), Y0["g2"] + NT + t
                    dve.wait_ge(y_done, y + 2)
                    own(nc.vector.reciprocal(rc[0:r, 0, 0:1], psY[y % Y_BANKS][0:r, D:D + 1]))
                    ts(tmp[0:r, 0, :], psY[y % Y_BANKS][0:r, 0:D], rc[0:r, 0, 0:1], 0.0, ALU.mult, ALU.max).then_inc(y_used, 1)
                    dve.wait_ge(y_used, Y_BANKS + y + 1)
                    own(tt(x[0:r, t, :], tmp[0:r, 0, :], x[0:r, t, :], ALU.add))

            block2(0)
            own(nc.vector.memset(V3[:, :, D:D + 1], 1.0))
            y = Y0["g2"]
            for t in range(NT):
                dve.wait_ge(y_done, y + 2)
                nc.vector.tensor_copy(V3[0:rows(t), t, 0:D], psY[y % Y_BANKS][0:rows(t), 0:D]).then_inc(y_used, 1)
                y += 1
            dve.wait_ge(y_used, Y_BANKS + y)
            dve.sem_inc(v_ready, 1)
            block2(1)
            take2(0)
            block2(2)
            take2(1)
            take2(2)
            layernorm(x, xn, "m_a")
            layernorm(xn, xh, "m_b")
            for i in range(2):
                last = nc.vector.memset(xcp[i][:, 0:TAPS - 1], 0.0)
            last.then_inc(pad_zero, 1)
            own(nc.vector.memset(carry[:, :], 0.0))
            for d in range(DB):
                dve.wait_ge(h_used, H_BANKS + H0["mamba_in"] + T_ITEMS + (d + 1) * NC)
                if d >= 2:
                    dve.wait_ge(xs_ready, d - 1)
                acc, src = cacc[d % 2], xcp[d % 2]
                own(ts(acc, src[:, 0:MN], mcw[:, d, 0:1], None, ALU.mult))
                for k in range(1, TAPS):
                    ins = stt(acc, src[:, k:k + MN], mcw[:, d, k:k + 1], acc, ALU.mult, ALU.add)
                    if k < TAPS - 1:
                        own(ins)
                    else:
                        ins.then_inc(conv_done, 1)
            with dve.Fori(0, NC) as c:
                m = [0]

                def mown(ins):
                    m[0] += 1
                    ins.then_inc(m_chain, 1)
                    dve.wait_ge(m_chain, c * M_CHAIN + m[0])

                dve.wait_ge(sp_ready, c + 1)
                mown(ts(dBx, delta[:, :, :], LOG1P[-1], None, ALU.mult))
                for coef in LOG1P[-2::-1]:
                    mown(stt(dBx, dBx, coef, delta[:, :, :], ALU.add, ALU.mult))
                mown(tt(delta[:, :, :], dBx, u[:, :, :], ALU.add))
                mown(tt(u[:, :, :], delta[:, :, :], xs[:, :, bass.ds(c * MW, MW)], ALU.mult))
                for n in range(DS):
                    dve.wait_ge(m_bc, c * DS + (n + 1))
                    mown(tt(dBx, u[:, :, :], wide(psB[n % 2][:, 0:MW], DB, MW), ALU.mult))
                    dve.wait_ge(m_dA, c * DS + (n + 1))
                    for d in range(DB):
                        last = nc.vector.tensor_tensor_scan(hS[:, d, :], dA[n % 2][:, d, :], dBx[:, d, :],
                                                            carry[:, n * DB + d:n * DB + d + 1], ALU.mult, ALU.add)
                    mown(last)
                    nc.vector.tensor_copy(carry[:, n * DB:(n + 1) * DB], hS[:, :, MW - 1])
                    if n >= 2:
                        dve.wait_ge(m_acc, c * DS + (n - 1))
                    tt(hC[n % 2], hS, wide(psC[n % 2][:, 0:MW], DB, MW), ALU.mult).then_inc(m_hc, 1)
                dve.wait_ge(m_acc, c * DS + DS)
                for d in range(DB):
                    last = stt(dBx[:, d, :], xs[:, d, bass.ds(c * MW, MW)], mds[:, d:d + 1],
                               psH[(H0["mamba_scan"] + d) % H_BANKS][:, 0:MW], ALU.mult, ALU.add)
                mown(last)
                tt(xs[:, :, bass.ds(c * MW, MW)], dBx, zg[:, :, :], ALU.mult).then_inc(m_y, 1)
                assert m[0] == M_CHAIN
            first_weights_lo("f2", 0)
            for t in range(NT):
                r, y = rows(t), Y0["mamba_out"] + t
                dve.wait_ge(y_done, y + 2)
                tt(xh[0:r, t, :], psY[y % Y_BANKS][0:r, 0:D], xh[0:r, t, :], ALU.add).then_inc(y_used, 1)
            all_taken("f2")
            layernorm(xh, xh, "f2")
            own(nc.vector.memset(gates[:, :, 0:2], 0.5))
            own(tt(x[:, :, :], x[:, :, :], xn[:, :, 0:D], ALU.add))
            first_weights_lo("f2", 1)
            split_x("f2")
            ffn("f2")
            all_taken("g3")
            layernorm(x, xn, "g3")
            own(nc.vector.memset(xn[:, :, D:XC], 1.0))
            dve.wait_ge(a_done, 1)
            nc.vector.tensor_copy(g3r[:, :, D:D + 2], psM[0][:, 0:4].rearrange("p (k n) -> p k n", k=KD)).then_inc(a_used, 1)
            y = Y0["g3"]
            for t in range(NT):
                dve.wait_ge(y_done, y + 2)
                nc.vector.tensor_copy(V3[0:rows(t), t, 0:D + 2], psY[y % Y_BANKS][0:rows(t), 0:D + 2]).then_inc(y_used, 1)
                y += 1
            for t in range(NT):
                r = rows(t)
                dve.wait_ge(y_done, y + 2)
                nc.vector.tensor_copy(xn[0:r, t, 0:D], psY[y % Y_BANKS][0:r, 0:D])
                nc.vector.tensor_copy(xn[0:r, t, D + 1:XC], psY[y % Y_BANKS][0:r, D + 1:XC]).then_inc(y_used, 1)
                y += 1
            dve.wait_ge(y_used, Y_BANKS + y)
            dve.sem_inc(v_ready, 1)
            dve.wait_ge(h_used, H_BANKS + H0["g3"] + T_ITEMS + NC)
            dve.wait_ge(adj_again, DMA)

            def block3_(c):
                b, w = block3[c % 2][:, :, 0:CHUNK_W[c]], CHUNK_W[c]
                own(tt(b, wide(row[:, c * CW:c * CW + w], NT, w), xn[:, :, D + 1:D + 2].broadcast_to([P, NT, w]), ALU.add))
                stt(b, b, 0.01, b, ALU.mult, ALU.max).then_inc(blk_raw, 1)

            def mask3(c):
                b, w = block3[c % 2][:, :, 0:CHUNK_W[c]], CHUNK_W[c]
                dve.wait_ge(blk_exp, NC + c + 1)
                stt(b, adj3[:, :, c * CW:c * CW + w], 0.0, b, ALU.not_equal, ALU.mult).then_inc(blk, 1)

            ya = y

            def take_b(tiles):
                for t in tiles:
                    r, y = rows(t), ya + t
                    dve.wait_ge(y_done, y + 2)
                    tt(sig[0:r, t, :], psY[y % Y_BANKS][0:r, D:D + 2], xn[0:r, t, D + 2:D + 4], ALU.add)
                    tt(XB[0:r, t, :], psY[y % Y_BANKS][0:r, 0:D], bias3[0:r, :], ALU.add).then_inc(y_used, 1)

            def take_a(c):
                for t in CHUNK_T[c]:
                    r, y = rows(t), ya + NT + t
                    dve.wait_ge(y_done, y + 2)
                    own(ts(rc[0:r, t % 2, 0:1], psY[y % Y_BANKS][0:r, D:D + 1], EPS, None, ALU.add))
                    own(nc.vector.reciprocal(rc[0:r, t % 2, 1:2], rc[0:r, t % 2, 0:1]))
                    ts(XB[0:r, t, :], XB[0:r, t, :], sig[0:r, t, 1:2], None, ALU.mult)
                    own(ts(rc[0:r, t % 2, 0:1], rc[0:r, t % 2, 1:2], sig[0:r, t, 0:1], None, ALU.mult))
                    stt(XB[0:r, t, :], psY[y % Y_BANKS][0:r, 0:D], rc[0:r, t % 2, 0:1], XB[0:r, t, :], ALU.mult, ALU.add).then_inc(y_used, 1)

            own(nc.vector.memset(sig[:, :, :], 0.0))
            block3_(0)
            take_b(range(0, 4))
            mask3(0)
            block3_(1)
            take_b(range(4, NT))
            dve.wait_ge(y_used, Y_BANKS + ya + NT)
            own(tt(sig[:, :, :], sig[:, :, :], wide(bab[:, :], NT, 2), ALU.add))
            dve.sem_inc(za_ready, 1)
            mask3(1)
            dve.wait_ge(za_sig, 1)
            take_a(0)
            block3_(2)
            mask3(2)
            take_a(1)
            first_weights_lo("f3", 0)
            take_a(2)
            dve.wait_ge(y_used, Y_BANKS + Y0["t_f3"])
            dve.sem_inc(fin_ready, 1)
            dve.wait_ge(fin_sig, 1)
            tt(x[:, 0:NT - 1, :], x[:, 0:NT - 1, :], XB[:, 0:NT - 1, :], ALU.add)
            own(tt(x[0:LAST, NT - 1, :], x[0:LAST, NT - 1, :], XB[0:LAST, NT - 1, :], ALU.add))
            layernorm(x, xn, "f3")
            first_weights_lo("f3", 1)
            split_x("f3")
            gating("f3", False, True)
            ffn("f3")


N_CONST = 14
LOG1P = (1.0, -0.4999950151678741, 0.33319271342508366, -0.24844369892516138, 0.1911143108072622,
         -0.13674769705756462, 0.07836166802050314, -0.02958850739350184, 0.005253457797072649)
M_CHAIN = len(LOG1P) + 2 + 2 * DS + 1


def kernel(**inputs):
    import numpy as np
    import concourse.bacc as bacc
    from concourse.bass_utils import run_bass_kernel_spmd

    i = {k: np.asarray(v) for k, v in inputs.items()}
    f = np.float32

    def blocks(w, axis=0):
        return np.moveaxis(w.reshape(w.shape[0] // P, P, *w.shape[1:]), 0, 1)

    def experts(w):
        e, r, n = w.shape
        return w.reshape(e, r // P, P, n).transpose(0, 2, 1, 3).reshape(e, P, r // P * n)

    def hidden_bias(b):
        e, n = b.shape
        return b.reshape(e, n // P, P).transpose(0, 2, 1)

    xp = np.zeros((NT * P, D), f)
    xp[:N] = i["x"]
    adj = np.zeros((NT * P, N), f)
    adj[:N] = i["adj"].T
    g3sa = i["L3_gnn_W_sa"]
    wa, wb = i["L3_gnn_Wa"][0], i["L3_gnn_Wb"][0]
    arrays = {
        "x": blocks(xp), "adj": blocks(adj),
        "ident": np.eye(P, dtype=f), "ones": np.ones((P, P), f),
        "before": np.tile(np.tril(np.ones((8, 8), f), -1).reshape(1, 64), (P, 1)),
        "wgate": np.stack([blocks(i["L0_ffn_Wg"]), blocks(i["L1_ffn_gate_w"].T), blocks(i["L3_ffn_Wr"])], 1),
        "bnode": blocks(i["L2_gnn_b_node"]),
        "mcw": blocks(i["L2_ffn_conv_w"][:, 0, :]), "mcb": blocks(i["L2_ffn_conv_b"]), "mdb": blocks(i["L2_ffn_dt_proj_b"]),
        "mds": blocks(i["L2_ffn_D_skip"]),
        "malog": blocks(i["L2_ffn_A_log"]).transpose(0, 2, 1).reshape(P, DB * DS),
        "bias0": i["L0_gnn_b"].reshape(1, D), "bias3": i["L3_gnn_b_gcnb"].reshape(1, D),
        "bgate": i["L1_ffn_gate_b"].reshape(1, 8), "bab": np.concatenate([i["L3_gnn_ba"], i["L3_gnn_bb"]]).reshape(1, 2),
        "g0w": blocks(i["L0_gnn_W"]), "g2n": blocks(i["L2_gnn_W_node"]),
        "g2k": np.stack([blocks(k) for k in i["L2_gnn_K"]], 1),
        "g3sa": blocks(g3sa), "g3t": blocks(g3sa.T), "g3a": blocks(i["L3_gnn_a_sa"].reshape(2, D).T),
        "g3x": blocks(np.stack([wa[D:], wb[D:]], 1)),
        "g3l": blocks(np.concatenate([i["L3_gnn_W_gcnb"], wa[:D, None], wb[:D, None]], 1)),
        "mwin": blocks(i["L2_ffn_in_proj_w"].T), "mwx": blocks(i["L2_ffn_x_proj_w"].T),
        "mwdt": i["L2_ffn_dt_proj_w"].T, "mwo": blocks(i["L2_ffn_out_proj_w"].T),
        "w1_0": experts(i["L0_ffn_W1"]), "w2_0": experts(i["L0_ffn_W2"]), "b1_0": hidden_bias(i["L0_ffn_b1"]), "b2_0": i["L0_ffn_b2"],
        "w1_1": experts(np.concatenate([i["L1_ffn_rw1"], i["L1_ffn_sw1"]]).transpose(0, 2, 1)),
        "w2_1": experts(np.concatenate([i["L1_ffn_rw2"], i["L1_ffn_sw2"]]).transpose(0, 2, 1)),
        "b1_1": hidden_bias(np.concatenate([i["L1_ffn_rb1"], i["L1_ffn_sb1"]])),
        "b2_1": np.concatenate([i["L1_ffn_rb2"], i["L1_ffn_sb2"]]),
        "w1_2": experts(i["L2_ffn_moe_w1"].transpose(0, 2, 1)), "w2_2": experts(i["L2_ffn_moe_w2"].transpose(0, 2, 1)),
        "b1_2": hidden_bias(i["L2_ffn_moe_b1"]), "b2_2": i["L2_ffn_moe_b2"],
        "w1_3": experts(i["L3_ffn_W1"]), "w2_3": experts(i["L3_ffn_W2"]), "b1_3": hidden_bias(i["L3_ffn_b1"]), "b2_3": i["L3_ffn_b2"],
    }
    nc = bacc.Bacc("TRN2", target_bir_lowering=False, num_devices=1)
    feed, args = {}, {}
    for name, v in arrays.items():
        v = np.ascontiguousarray(v)
        feed[f"in_{name}"] = v
        args[name] = nc.dram_tensor(f"in_{name}", v.shape, F32, kind="ExternalInput").ap()
    out = nc.dram_tensor("out", (N, D), F32, kind="ExternalOutput").ap()
    build(nc, args, out)
    r = run_bass_kernel_spmd(nc, [feed], core_ids=[0])
    return r.results[0]["out"]
```

```python
from contextlib import ExitStack

import concourse.bass as bass
from concourse import mybir

F32 = mybir.dt.float32
F16 = mybir.dt.float16
ALU = mybir.AluOpType
ACT = mybir.ActivationFunctionType
AX_X = mybir.AxisListType.X

P = 128
N = 1354
D = 256
KD = D // P
NT = -(-N // P)
LAST = N - (NT - 1) * P
CW = 512
NC = -(-N // CW)
TPC = CW // P
XC = D + 4
DI = 512
DB = DI // P
DS = 16
DR = 16
TAPS = 4
VB = 2
MW = 452
MN = NC * MW
EPS = 1e-5
NEG = -10000000000.0
H_BANKS, Y_BANKS = 4, 2

CHUNK_W = [min(CW, N - c * CW) for c in range(NC)]
CHUNK_T = [range(c * TPC, min((c + 1) * TPC, NT)) for c in range(NC)]


def rows(t):
    return P if t < NT - 1 else LAST


FFN = {"f0": (8, 4), "f1": (10, 8), "f2": (2, 4), "f3": (8, 8)}
T_ITEMS = KD * NC
STAGES = [
    ("g0", T_ITEMS, 2 * NT),
    ("t_f0", T_ITEMS, 0),
    ("f0", 8 * NC * 4, 8 * NT),
    ("g1", 0, NT),
    ("t_f1", T_ITEMS, 0),
    ("f1", 10 * NC * 8, 10 * NT),
    ("g2", 2 * T_ITEMS, 2 * NT),
    ("mamba_in", T_ITEMS + DB * NC + NC, 0),
    ("mamba_scan", NC * 2 * DB, 0),
    ("mamba_out", 0, NT),
    ("t_f2", T_ITEMS, 0),
    ("f2", 2 * NC * 4, 2 * NT),
    ("g3", T_ITEMS + NC, 4 * NT),
    ("t_f3", T_ITEMS, 0),
    ("f3", 8 * NC * 8, 8 * NT),
]
H0, Y0 = {}, {}
_h = _y = 0
for _name, _nh, _ny in STAGES:
    H0[_name], Y0[_name] = _h, _y
    _h, _y = _h + _nh, _y + _ny
Y_END = _y
LOADS0 = {"f0": 0, "f1": 8, "f2": 18, "f3": 20}
XS, WS, HS = 256.0, 256.0, 64.0
PIECE = 1024
PIECES = {k: 2 * fb * KD * P // PIECE for k, (_, fb) in FFN.items()}
PIECE0, ITEM0 = {}, {}
_p = _i = 0
for _name, (_e, _fb) in FFN.items():
    PIECE0[_name], ITEM0[_name] = _p, _i
    _p, _i = _p + _e * PIECES[_name], _i + _e * NC * _fb
X_SPLIT0 = {"f0": 0, "f1": 1, "f2": 2, "f3": 3}
LN = {n: i for i, n in enumerate(["g0", "f0", "g1", "f1", "g2", "m_a", "m_b", "f2", "g3", "f3"])}
GROUPS = [range(0, 2 * TPC), range(2 * TPC, NT)]
GROUP_C = [range(0, 2), range(2, NC)]
J_GROUPS = [(0, 6), (6, NT)]


def ln_count(ln, g):
    if ln in ("m_a", "m_b"):
        return 2 * LN["m_a"] + 2 * g + (1 if ln == "m_a" else 2)
    return 2 * LN[ln] + g + 1


GATE = {"f0": 0, "f1": 1, "f3": 2}
DMA = 16


def build(nc, a, out):
    ctx = ExitStack()
    with ctx:
        def sb(name, shape):
            return ctx.enter_context(nc.sbuf_tensor(name, shape, F32))

        def sb16(name, shape):
            return ctx.enter_context(nc.sbuf_tensor(name, shape, F16))

        def sem(name):
            return ctx.enter_context(nc.semaphore(name))

        x = sb("x", [P, NT, D])
        xn = sb("xn", [P, NT, XC])
        xT = sb("xT", [P, KD * NT * P])
        adjT = sb("adjT", [P, NT * N])
        wparts = sb16("wparts", [P, 2, 2, 2, 8 * D])
        stage = sb("stage", [P, 2, PIECE])
        b1 = sb("b1", [P, 2, 8])
        b2 = sb("b2", [P, 2, D])
        work = sb("work", [P, 2 * NT * CW])
        V = sb("V", [P, NT * XC])
        row = sb("row", [P, MN])
        gw = sb("gw", [P, KD * D])
        ident = sb("ident", [P, P])
        ones = sb("ones", [P, 2])
        before = sb("before", [P, 64])
        bias0 = sb("bias0", [P, D])
        bias3 = sb("bias3", [P, D])
        wgate = sb("wgate", [P, 3, KD, 8])
        bgate = sb("bgate", [P, 8])
        bnode = sb("bnode", [P, KD])
        bab = sb("bab", [P, 2])
        mcw = sb("mcw", [P, DB, TAPS])
        mcb = sb("mcb", [P, DB])
        mdb = sb("mdb", [P, DB])
        mds = sb("mds", [P, DB])
        malog = sb("malog", [P, DB * DS])
        mA = sb("mA", [P, DB * DS])
        carry = sb("carry", [P, DB * DS])
        dbcc = sb("dbcc", [48, MW])
        gates = sb("gates", [P, NT, 10])
        gates_s = sb("gates_s", [P, NT, 10])
        lg = sb("lg", [P, NT, 8])
        pr = sb("pr", [P, NT, 8])
        rank = sb("rank", [P, NT, 8])
        gmx = sb("gmx", [P, NT])
        gsum = sb("gsum", [P, NT])
        st = sb("st", [P, NT, 6])
        mv = sb("mv", [P, NT, 2])
        var = sb("var", [P, NT])
        std = sb("std", [P, NT])
        rstd = sb("rstd", [P, NT])
        deg = sb("deg", [P, NT])
        dsq = sb("dsq", [P, NT])
        dinv = sb("dinv", [P, NT])
        sig = sb("sig", [P, NT, 2])
        rc = sb("rc", [P, 2, 2])
        tmp = sb("tmp", [P, 2, D])

        xT3 = xT[:, :].rearrange("p (k n) -> p k n", k=KD)
        adj3 = adjT[:, :].rearrange("p (j n) -> p j n", j=NT)
        V3 = V[:, :].rearrange("p (j n) -> p j n", j=NT)
        block3 = [work[:, h * NT * CW:(h + 1) * NT * CW].rearrange("p (j n) -> p j n", j=NT) for h in range(2)]
        hT = {fb: [[work[:, h * fb * CW:(h + 1) * fb * CW].bitcast(F16)[:, q * fb * CW:(q + 1) * fb * CW]
                    .rearrange("p (f n) -> p f n", f=fb) for q in range(2)] for h in range(2)] for fb in (4, 8)}
        x16 = [work[:, 8192:8192 + KD * NT * P].bitcast(F16)[:, q * KD * NT * P:(q + 1) * KD * NT * P]
               .rearrange("p (k n) -> p k n", k=KD) for q in range(2)]
        hraw = xn[:, :, :].rearrange("p t n -> p (t n)")[:, 0:4 * CW].rearrange("p (r n) -> p r n", r=4)
        cnt = work[:, 4096:4096 + N]
        mxp = work[:, 4096 + N:4096 + 2 * N]
        cmp = [V[:, N + 704 * i:N + 704 * (i + 1)] for i in range(2)]
        nB = V[:, 0:N]
        g0w = gw[:, 0:KD * D].rearrange("p (k n) -> p k n", k=KD)
        g2n = gw[:, 0:KD * D].rearrange("p (k n) -> p k n", k=KD)
        spare = block3[1].rearrange("p j n -> p (j n)")
        g2k = spare[:, 3072:3072 + 4 * KD * D].rearrange("p (h k n) -> p h k n", h=4, k=KD)
        g3r = spare[:, 0:KD * XC].rearrange("p (k n) -> p k n", k=KD)
        g3l = spare[:, 520:520 + KD * XC].rearrange("p (k n) -> p k n", k=KD)
        g3t = spare[:, 1040:1040 + KD * D].rearrange("p (k n) -> p k n", k=KD)
        g3a = spare[:, 1552:1552 + 4].rearrange("p (k n) -> p k n", k=KD)
        uT3 = spare[:, 0:3072].rearrange("p (k n) -> p k n", k=KD)
        xs = adjT[:, 0:DB * MN].rearrange("p (d n) -> p d n", d=DB)
        o = DB * MN
        delta, u, zg = [adjT[:, o + i * DB * MW:o + (i + 1) * DB * MW].rearrange("p (d n) -> p d n", d=DB)
                        for i in range(3)]
        o += 3 * DB * MW
        mwin = adjT[:, o:o + KD * 1024].rearrange("p (k n) -> p k n", k=KD)
        mwx = adjT[:, o + 2048:o + 2048 + DB * 48].rearrange("p (k n) -> p k n", k=DB)
        mwdt = adjT[0:DR, o + 2240:o + 2240 + DI]
        mwo = adjT[:, o + 2752:o + 2752 + DB * D].rearrange("p (k n) -> p k n", k=DB)
        xcp = [work[:, i * 1360:i * 1360 + TAPS - 1 + MN] for i in range(2)]
        cacc = [work[:, (2 + i) * 1360:(2 + i) * 1360 + MN] for i in range(2)]
        q = DB * MW
        dA = [work[:, i * q:(i + 1) * q].rearrange("p (d n) -> p d n", d=DB) for i in range(2)]
        hC = [work[:, (2 + i) * q:(3 + i) * q].rearrange("p (d n) -> p d n", d=DB) for i in range(2)]
        dBx0 = work[:, 4 * q:5 * q].rearrange("p (d n) -> p d n", d=DB)
        hS0 = work[:, 5 * q:6 * q].rearrange("p (d n) -> p d n", d=DB)
        free = wparts[:, :, :, :, :].rearrange("p s w q n -> p (s w q n)").bitcast(F32)
        dBx = [dBx0, free[:, 0:q].rearrange("p (d n) -> p d n", d=DB)]
        hS = [hS0, free[:, q:2 * q].rearrange("p (d n) -> p d n", d=DB)]
        Bs, Cs = [[free[:, 2 * q + (2 * i + j) * MW:2 * q + (2 * i + j + 1) * MW] for i in range(4)] for j in range(2)]
        dbc = row[0:48, 0:MN]
        xh = V[:, 0:NT * D].rearrange("p (j n) -> p j n", j=NT)
        XB = xT[:, 0:NT * D].rearrange("p (j n) -> p j n", j=NT)

        psH = [ctx.enter_context(nc.psum_tensor(f"psH{i}", [P, 512], F32)) for i in range(H_BANKS)]
        psY = [ctx.enter_context(nc.psum_tensor(f"psY{i}", [P, 512], F32)) for i in range(Y_BANKS)]
        psM = [ctx.enter_context(nc.psum_tensor(f"psM{i}", [P, 512], F32)) for i in range(2)]
        psB, psC = psY, psM

        x_in = sem("x_in")
        adj_in = [sem(f"adj_in{j}") for j in range(NT)]
        ident_in = sem("ident_in")
        ones_set = sem("ones_set")
        const_in = sem("const_in")
        g0_in = sem("g0_in")
        gw_in = sem("gw_in")
        gk_in = sem("gk_in")
        mw_in = sem("mw_in")
        adj_again = sem("adj_again")
        b_in = [sem(f"b_in{s}") for s in range(2)]
        st_in = [sem(f"st_in{s}") for s in range(2)]
        w_hi = sem("w_hi")
        w_split = sem("w_split")
        x_hi = sem("x_hi")
        x_split = sem("x_split")
        h_hi = sem("h_hi")
        h_split = sem("h_split")
        h_done = sem("h_done")
        h_used = sem("h_used")
        y_done = sem("y_done")
        y_used = sem("y_used")
        chain = sem("chain")
        ln_var = sem("ln_var")
        ln_std = sem("ln_std")
        ln_out = sem("ln_out")
        g_done = sem("g_done")
        g_shift = sem("g_shift")
        g_exp = sem("g_exp")
        b_added = sem("b_added")
        part_done = sem("part_done")
        all_done = sem("all_done")
        cnt_root = sem("cnt_root")
        deg_done = sem("deg_done")
        deg_max = sem("deg_max")
        deg_root = sem("deg_root")
        v_ready = sem("v_ready")
        blk_raw = sem("blk_raw")
        blk_exp = sem("blk_exp")
        blk = sem("blk")
        kmean = sem("kmean")
        a_done = sem("a_done")
        a_used = sem("a_used")
        za_ready = sem("za_ready")
        za_sig = sem("za_sig")
        fin_ready = sem("fin_ready")
        fin_sig = sem("fin_sig")
        act_chain = sem("act_chain")
        pad_zero = sem("pad_zero")
        conv_done = sem("conv_done")
        xs_ready = sem("xs_ready")
        sp_ready = sem("sp_ready")
        m_dA = sem("m_dA")
        m_bc = sem("m_bc")
        m_bcs = sem("m_bcs")
        m_db = sem("m_db")
        m_h = sem("m_h")
        m_hc = sem("m_hc")
        m_hcp = sem("m_hcp")
        m_acc = sem("m_acc")
        m_dbc = sem("m_dbc")
        m_chain = sem("m_chain")
        m_y = sem("m_y")
        out_done = sem("out_done")

        block = ctx.enter_context(nc.Block())

        @block.sync
        def _(sp):
            sp.dma_start(x[:, :, :], a["x"]).then_inc(x_in, DMA)
            sp.dma_start(ident[:, :], a["ident"]).then_inc(ident_in, DMA)
            sp.dma_start(g0w, a["g0w"]).then_inc(g0_in, DMA)
            for j in range(NT):
                sp.dma_start(adj3[:, j, :], a["adj"][:, j, :]).then_inc(adj_in[j], DMA)

            def load_expert(stage_, e, slot, q):
                k, n = stage_[1], PIECES[stage_]
                fb = FFN[stage_][1]
                sp.dma_start(b1[:, slot, 0:fb], a[f"b1_{k}"][bass.ds(e, 1)].rearrange("a p f -> (a p) f")).then_inc(b_in[slot], DMA)
                sp.dma_start(b2[:, slot, :], a[f"b2_{k}"][bass.ds(e, 1)].broadcast_to([P, D])).then_inc(b_in[slot], DMA)
                for i in range(n):
                    w = a[f"w{1 + i // (n // 2)}_{k}"][bass.ds(e, 1)].rearrange("a p f -> (a p) f")
                    o_ = i % (n // 2) * PIECE
                    sp.wait_ge(w_split, q + (i + 1))
                    sp.dma_start(stage[:, i % 2, :], w[:, o_:o_ + PIECE]).then_inc(st_in[i % 2], DMA)

            def load_first(stage_, before_stage):
                for s in range(2):
                    if before_stage:
                        n = FFN[before_stage][0]
                        sp.wait_ge(y_used, Y_BANKS + Y0[before_stage] + NT * (n - 1 + s))
                    load_expert(stage_, s, s, PIECE0[stage_] + s * PIECES[stage_])

            def load_rest(stage_):
                n = FFN[stage_][0]
                with sp.Fori(1, n // 2) as pair:
                    for s in range(2):
                        sp.wait_ge(y_used, pair * 2 * NT + (Y_BANKS + Y0[stage_] + NT * (s - 1)))
                        load_expert(stage_, pair * 2 + s, s, pair * (2 * PIECES[stage_]) + (PIECE0[stage_] + s * PIECES[stage_]))

            load_first("f0", None)
            load_rest("f0")
            load_first("f1", "f0")
            load_rest("f1")
            load_first("f2", "f1")
            load_first("f3", "f2")
            load_rest("f3")
            sp.wait_ge(y_used, Y_BANKS + Y_END)
            sp.dma_start(out[0:(NT - 1) * P, :].rearrange("(t p) d -> p t d", p=P), x[:, 0:NT - 1, :]).then_inc(out_done, DMA)
            sp.dma_start(out[(NT - 1) * P:N, :], x[0:LAST, NT - 1, :]).then_inc(out_done, DMA)
            sp.wait_ge(out_done, 2 * DMA)

        @block.gpsimd
        def _(pool):
            n_const = 0
            for dst, key in ((before[:, :], "before"), (wgate[:, :, :, :], "wgate"),
                             (bnode[:, :], "bnode"), (mcw[:, :, :], "mcw"), (mcb[:, :], "mcb"), (mdb[:, :], "mdb"),
                             (mds[:, :], "mds"), (malog[:, :], "malog")):
                pool.dma_start(dst, a[key]).then_inc(const_in, DMA)
                n_const += 1
            for dst, key, w in ((bias0[:, :], "bias0", D), (bias3[:, :], "bias3", D), (bgate[:, :], "bgate", 8), (bab[:, :], "bab", 2)):
                pool.dma_start(dst, a[key].broadcast_to([P, w])).then_inc(const_in, DMA)
                n_const += 1
            assert n_const == N_CONST
            pool.wait_ge(part_done, 1)
            pool.wait_ge(y_used, Y_BANKS + Y0["f0"])
            pool.partition_all_reduce(nB, cnt, P, bass.bass_isa.ReduceOp.add).then_inc(all_done, 1)
            pool.partition_all_reduce(row[:, 0:N], mxp, P, bass.bass_isa.ReduceOp.max).then_inc(all_done, 1)
            pool.dma_start(g2n, a["g2n"]).then_inc(gw_in, DMA)
            pool.wait_ge(y_used, Y_BANKS + Y0["g2"])
            pool.dma_start(g2k, a["g2k"]).then_inc(gk_in, DMA)
            pool.wait_ge(blk_exp, 2 * NC)
            for dst, key in ((mwin, "mwin"), (mwx, "mwx"), (mwdt, "mwdt"), (mwo, "mwo")):
                pool.dma_start(dst, a[key]).then_inc(mw_in, DMA)
            pool.sem_inc(m_hcp, 2)
            mul = nc.gpsimd.tensor_tensor

            def every(ap):
                return ap.rearrange("p (o n) -> p o n", o=1).broadcast_to([P, DB - VB, MW])

            pool.wait_ge(w_hi, PIECE0["f2"])
            pool.wait_ge(w_split, 2 + PIECE0["f2"])
            with pool.Fori(0, NC) as c:
                def times_b(n):
                    pool.wait_ge(m_bcs, c * DS + (n + 3))
                    if n >= 2:
                        pool.wait_ge(m_h, c * DS + (n - 1))
                    mul(dBx[n % 2][:, VB:DB, :], u[:, VB:DB, :], every(Bs[n % 4]), ALU.mult).then_inc(m_db, 1)

                pool.wait_ge(m_chain, c * M_CHAIN + (len(LOG1P) + 2))
                times_b(0)
                for n in range(DS):
                    if n + 1 < DS:
                        times_b(n + 1)
                    pool.wait_ge(m_h, c * DS + (n + 1))
                    if n >= 2:
                        pool.wait_ge(m_acc, c * DS + (n - 1))
                    mul(hC[n % 2][:, VB:DB, :], hS[n % 2][:, VB:DB, :], every(Cs[n % 4]), ALU.mult).then_inc(m_hcp, 1)
            pool.wait_ge(y_used, Y_BANKS + Y0["f2"])
            pool.dma_start(adjT[:, :], a["adj"].rearrange("p j n -> p (j n)")).then_inc(adj_again, DMA)
            pool.wait_ge(y_used, Y_BANKS + Y0["g3"])
            for dst, key in ((g3t, "g3t"), (g3a, "g3a"), (g3l[:, :, 0:D + 2], "g3l"), (g3r[:, :, 0:D], "g3sa"),
                             (g3r[:, :, D + 2:D + 4], "g3x")):
                pool.dma_start(dst, a[key]).then_inc(gw_in, DMA)
            pool.wait_ge(adj_again, DMA)

        @block.tensor
        def _(pe):
            pe.sem_inc(y_done, 1)
            pe.wait_ge(ident_in, DMA)

            def transposes(src, stage, ln):
                i = H0[stage]
                for g, chunks in enumerate(GROUP_C):
                    pe.wait_ge(ln_out, ln_count(ln, g))
                    for c in chunks:
                        for k in range(KD):
                            pe.wait_ge(h_used, i + 1)
                            for n, t in enumerate(CHUNK_T[c]):
                                last = nc.tensor.transpose(psH[i % H_BANKS][:, n * P:(n + 1) * P],
                                                           src[:, t, k * P:(k + 1) * P], ident[:, :])
                            last.then_inc(h_done, 1)
                            i += 1
                pe.wait_ge(h_used, H_BANKS + i)

            def gate_logits(stage):
                g = GATE[stage]
                for t in range(NT):
                    for k in range(KD):
                        last = nc.tensor.matmul(psM[0][:, t * 8:(t + 1) * 8], xT3[:, k, t * P:(t + 1) * P],
                                                wgate[:, g, k, :], start=(k == 0), stop=(k == KD - 1))
                last.then_inc(g_done, 1)

            def ffn(stage):
                experts, fb = FFN[stage]
                h0, y0, i0 = H0[stage], Y0[stage], ITEM0[stage]
                per_h, per_y, per_w = 2 * NC * fb, 2 * NT, 2 * PIECES[stage]
                parts = ((0, 0), (0, 1), (1, 0))
                pe.wait_ge(x_split, X_SPLIT0[stage] + 1)

                def body(pair):
                    def hidden(s, c):
                        for f in range(fb):
                            i = (s * NC + c) * fb + f
                            pe.wait_ge(h_used, pair * per_h + (h0 + i + 1))
                            for k in range(KD):
                                for wq, xq in parts:
                                    last = nc.tensor.matmul(psH[(h0 + i) % H_BANKS][:, 0:CHUNK_W[c]],
                                                            wparts[:, s, 0, wq, (k * fb + f) * P:(k * fb + f + 1) * P],
                                                            x16[xq][:, k, c * CW:c * CW + CHUNK_W[c]],
                                                            start=(k == wq == xq == 0), stop=(k == KD - 1 and wq == 1))
                            last.then_inc(h_done, 1)

                    def output(s, c):
                        pe.wait_ge(h_split, pair * (per_h // 2) + (2 + (i0 + (s * NC + c + 1) * fb) // 2))
                        for n, t in enumerate(CHUNK_T[c]):
                            i = s * NT + t
                            pe.wait_ge(y_used, pair * per_y + (y0 + i + 1))
                            for f in range(fb):
                                for hq, wq in parts:
                                    last = nc.tensor.matmul(psY[(y0 + i) % Y_BANKS][0:rows(t), 0:D],
                                                            hT[fb][(s * NC + c) % 2][hq][:, f, n * P:n * P + rows(t)],
                                                            wparts[:, s, 1, wq, f * D:(f + 1) * D],
                                                            start=(f == hq == wq == 0), stop=(f == fb - 1 and hq == 1))
                            last.then_inc(y_done, 1)

                    order = [(s, c) for s in range(2) for c in range(NC)]
                    for n, (s, c) in enumerate(order):
                        if c == 0:
                            pe.wait_ge(w_split, pair * per_w + (2 + PIECE0[stage] + s * PIECES[stage] + PIECES[stage] // 2))
                        hidden(s, c)
                        if c == 0:
                            pe.wait_ge(w_split, pair * per_w + (2 + PIECE0[stage] + (s + 1) * PIECES[stage]))
                        if n:
                            output(*order[n - 1])
                    output(*order[-1])

                if experts > 2:
                    with pe.Fori(0, experts // 2 - 1) as pair:
                        body(pair)
                body(experts // 2 - 1)

            def attend(y, tiles, src, off, values, cols, built=None, before=0):
                for t in tiles:
                    pe.wait_ge(y_used, y + 1)
                    for j in range(NT):
                        if built is not None and t == tiles[0] and j in (J_GROUPS[0][0], J_GROUPS[1][0]):
                            pe.wait_ge(built, before + 1 + (j > 0))
                        last = nc.tensor.matmul(psY[y % Y_BANKS][0:rows(t), 0:cols],
                                                src[0:rows(j), j, t * P - off:t * P - off + rows(t)],
                                                values[0:rows(j), j, 0:cols], start=(j == 0), stop=(j == NT - 1))
                    last.then_inc(y_done, 1)
                    y += 1
                return y

            def project(y, src3, w3, blocks, cols):
                for t in range(NT):
                    pe.wait_ge(y_used, y + 1)
                    for k in range(blocks):
                        last = nc.tensor.matmul(psY[y % Y_BANKS][0:rows(t), 0:cols], src3[:, k, t * P:t * P + rows(t)],
                                                w3[:, k, 0:cols], start=(k == 0), stop=(k == blocks - 1))
                    last.then_inc(y_done, 1)
                    y += 1
                return y

            transposes(xn, "g0", "g0")
            pe.wait_ge(ones_set, 1)
            for j in range(NT):
                pe.wait_ge(adj_in[j], DMA)
                for t in range(NT):
                    last = nc.tensor.matmul(psM[1][0:rows(t), t:t + 1], adj3[0:rows(j), j, t * P:t * P + rows(t)], ones[0:rows(j), 0:1],
                                            start=(j == t == 0), stop=(j == t == NT - 1), skip_group_check=True)
            last.then_inc(deg_done, 1)
            pe.wait_ge(g0_in, DMA)
            y = project(Y0["g0"], xT3, g0w, KD, D)
            pe.wait_ge(v_ready, 1)
            attend(y, range(NT), adj3, 0, V3, D)
            transposes(xn, "t_f0", "f0")
            pe.wait_ge(const_in, DMA * N_CONST)
            gate_logits("f0")
            ffn("f0")
            pe.wait_ge(ln_out, 2 * LN["g1"] + 2)
            y = Y0["g1"]
            for c in range(NC):
                y = attend(y, CHUNK_T[c], block3[c % 2], c * CW, xn, D + 1, blk, 2 * c)
            transposes(V3, "t_f1", "f1")
            gate_logits("f1")
            ffn("f1")
            transposes(xn, "g2", "g2")
            pe.wait_ge(gw_in, DMA)
            i = H0["g2"] + T_ITEMS
            for k2 in range(KD):
                for c in range(NC):
                    pe.wait_ge(h_used, i + 1)
                    for k in range(KD):
                        last = nc.tensor.matmul(psH[i % H_BANKS][:, 0:CHUNK_W[c]], g2n[:, k, k2 * P:(k2 + 1) * P],
                                                xT3[:, k, c * CW:c * CW + CHUNK_W[c]], start=(k == 0), stop=(k == KD - 1))
                    last.then_inc(h_done, 1)
                    i += 1
            pe.wait_ge(h_used, H_BANKS + i)
            pe.wait_ge(kmean, 1)
            y = project(Y0["g2"], uT3, g2k[:, 0], KD, D)
            pe.wait_ge(v_ready, 2)
            for c in range(NC):
                y = attend(y, CHUNK_T[c], block3[c % 2], c * CW, V3, D + 1, blk_exp, 2 * c)
            transposes(xh, "mamba_in", "m_b")
            pe.wait_ge(mw_in, 4 * DMA)
            i = H0["mamba_in"] + T_ITEMS
            for d in range(DB):
                for c in range(NC):
                    pe.wait_ge(h_used, i + 1)
                    for k in range(KD):
                        last = nc.tensor.matmul(psH[i % H_BANKS][:, 0:MW], mwin[:, k, d * P:(d + 1) * P],
                                                xT3[:, k, c * MW:(c + 1) * MW], start=(k == 0), stop=(k == KD - 1))
                    last.then_inc(h_done, 1)
                    i += 1
            pe.wait_ge(xs_ready, DB)
            for c in range(NC):
                pe.wait_ge(h_used, i + 1)
                for k in range(DB):
                    last = nc.tensor.matmul(psH[i % H_BANKS][0:48, 0:MW], mwx[:, k, :], xs[:, k, c * MW:(c + 1) * MW],
                                            start=(k == 0), stop=(k == DB - 1))
                last.then_inc(h_done, 1)
                i += 1
            pe.wait_ge(h_used, H_BANKS + i)
            with pe.Fori(0, NC) as c:
                i = H0["mamba_scan"]
                for d in range(DB):
                    pe.wait_ge(h_used, c * (2 * DB) + (i + 1))
                    if d == 0:
                        pe.wait_ge(m_y, c + 1)
                        pe.wait_ge(m_dbc, c + 1)
                    nc.tensor.matmul(psH[i % H_BANKS][:, 0:MW], mwdt[:, d * P:(d + 1) * P], dbcc[0:DR, :],
                                     start=True, stop=True).then_inc(h_done, 1)
                    i += 1
                for d in range(DB):
                    pe.wait_ge(h_used, c * (2 * DB) + (i + 1))
                    for k in range(KD):
                        last = nc.tensor.matmul(psH[i % H_BANKS][:, 0:MW], mwin[:, k, DI + d * P:DI + (d + 1) * P],
                                                xT3[:, k, bass.ds(c * MW, MW)], start=(k == 0), stop=(k == KD - 1))
                    last.then_inc(h_done, 1)
                    i += 1
                pe.wait_ge(h_used, c * (2 * DB) + (H_BANKS + i))

                def spread(n):
                    pe.wait_ge(m_bcs, c * DS + (n + 1))
                    nc.tensor.matmul(psB[n % 2][:, 0:MW], ident[0:48, DR + n:DR + n + 1].broadcast_to([48, P]),
                                     dbcc[:, :], start=True, stop=True)
                    nc.tensor.matmul(psC[n % 2][:, 0:MW], ident[0:48, DR + DS + n:DR + DS + n + 1].broadcast_to([48, P]),
                                     dbcc[:, :], start=True, stop=True).then_inc(m_bc, 1)

                for n in range(4):
                    spread(n)
                for n in range(DS):
                    if n + 4 < DS:
                        spread(n + 4)
                    pe.wait_ge(m_hcp, c * DS + (n + 3))
                    pe.wait_ge(m_hc, c * DS + (n + 3))
                    for d in range(DB):
                        last = nc.tensor.matmul(psH[(H0["mamba_scan"] + d) % H_BANKS][:, 0:MW], ident[:, :], hC[n % 2][:, d, :],
                                                start=(n == 0), stop=(n == DS - 1))
                    last.then_inc(m_acc, 1)
            pe.wait_ge(m_y, NC + 1)
            project(Y0["mamba_out"], xs, mwo, DB, D)
            transposes(xh, "t_f2", "f2")
            ffn("f2")
            transposes(xn, "g3", "g3")
            pe.wait_ge(gw_in, 6 * DMA)
            for k2 in range(KD):
                for k in range(KD):
                    last = nc.tensor.matmul(psM[0][:, 2 * k2:2 * k2 + 2], g3t[:, k, k2 * P:(k2 + 1) * P], g3a[:, k, :],
                                            start=(k == 0), stop=(k == KD - 1))
            last.then_inc(a_done, 1)
            y = project(Y0["g3"], xT3, g3l, KD, D + 2)
            pe.wait_ge(a_used, 1)
            i = H0["g3"] + T_ITEMS
            for c in range(NC):
                pe.wait_ge(h_used, i + 1)
                for k in range(KD):
                    last = nc.tensor.matmul(psH[i % H_BANKS][:, 0:CHUNK_W[c]], g3r[:, k, D:D + 1].broadcast_to([P, P]),
                                            xT3[:, k, c * CW:c * CW + CHUNK_W[c]], start=(k == 0), stop=(k == KD - 1))
                last.then_inc(h_done, 1)
                i += 1
            y = project(y, xT3, g3r, KD, XC)
            pe.wait_ge(v_ready, 3)
            pe.wait_ge(adj_again, DMA)
            y = attend(y, range(NT), adj3, 0, V3, D + 2)
            for c in range(NC):
                y = attend(y, CHUNK_T[c], block3[c % 2], c * CW, xn, D + 1, blk, 2 * (NC + c))
            transposes(V3, "t_f3", "f3")
            gate_logits("f3")
            ffn("f3")

        @block.scalar
        def _(act):
            act.sem_inc(h_used, H_BANKS)
            act.sem_inc(m_bcs, 2)
            n_own = [0]

            def own(ins):
                n_own[0] += 1
                ins.then_inc(act_chain, 1)
                act.wait_ge(act_chain, n_own[0])

            def ln_root(ln, groups=(0, 1)):
                for g in groups:
                    i = slice(GROUPS[g][0], GROUPS[g][-1] + 1)
                    act.wait_ge(ln_var, ln_count(ln, g))
                    nc.scalar.activation(std[:, i], var[:, i], ACT.Sqrt).then_inc(ln_std, 1)

            def take(i, dst, width, func=ACT.Copy, rows_=P, **kw):
                act.wait_ge(h_done, i + 1)
                nc.scalar.activation(dst, psH[i % H_BANKS][0:rows_, 0:width], func, **kw).then_inc(h_used, 1)

            def take_transposes(stage, split=False):
                i = H0[stage]
                for c in range(NC):
                    for k in range(KD):
                        w = len(CHUNK_T[c]) * P
                        if split:
                            act.wait_ge(h_done, i + 1)
                            last = nc.scalar.activation(x16[0][:, k, c * CW:c * CW + w], psH[i % H_BANKS][:, 0:w], ACT.Copy, scale=XS)
                            last.then_inc(x_hi, 1)
                        take(i, xT3[:, k, c * CW:c * CW + w], w)
                        i += 1

            def weights_hi(stage_, pair, e, i):
                n = PIECES[stage_]
                q = PIECE0[stage_] + e * n + i
                act.wait_ge(st_in[i % 2], pair * (n * DMA) + (q // 2 + 1) * DMA)
                dst = wparts[:, e % 2, i // (n // 2), 0, i % (n // 2) * PIECE:(i % (n // 2) + 1) * PIECE]
                nc.scalar.activation(dst, stage[:, i % 2, :], ACT.Copy, scale=WS).then_inc(w_hi, 1)

            def first_weights_hi(stage_, half):
                for i in range(2 * half, min(2 * half + 2, PIECES[stage_])):
                    weights_hi(stage_, 0, 0, i)

            def gate_exp(stage, scale):
                act.wait_ge(g_shift, GATE[stage] + 1)
                nc.scalar.activation(pr[:, :, :], lg[:, :, :], ACT.Exp, scale=scale).then_inc(g_exp, 1)

            def ffn(stage_, func, middle=None):
                experts, fb = FFN[stage_]
                h0, i0 = H0[stage_], ITEM0[stage_]

                def body(pair, last_pair):
                    for s in range(2):
                        act.wait_ge(b_in[s], pair * (2 * DMA) + 2 * DMA * (LOADS0[stage_] // 2 + 1))
                        for c in range(NC):
                            for f in range(fb):
                                i = (s * NC + c) * fb + f
                                if f % 2 == 0:
                                    act.wait_ge(h_split, pair * (NC * fb) + ((i0 + i) // 2 + 1))
                                act.wait_ge(h_done, pair * (2 * NC * fb) + (h0 + i + 1))
                                nc.scalar.activation(hraw[:, (i0 + i) % 4, 0:CHUNK_W[c]], psH[(h0 + i) % H_BANKS][:, 0:CHUNK_W[c]],
                                                     func, bias=b1[:, s, f:f + 1], scale=1.0 / (XS * WS)).then_inc(h_used, 1)
                                if f == 1:
                                    s2, c2 = divmod(s * NC + c - 2, NC)
                                    act.wait_ge(y_done, pair * (2 * NT) + (Y0[stage_] + s2 * NT + CHUNK_T[c2][-1] + 2))
                                if f % 2 == 1:
                                    act.wait_ge(h_used, pair * (2 * NC * fb) + (H_BANKS + h0 + i + 1))
                                    j = (i0 + i) % 4 - 1
                                    nc.scalar.activation(hT[fb][(s * NC + c) % 2][0][:, f - 1:f + 1, 0:CHUNK_W[c]],
                                                         hraw[:, j:j + 2, 0:CHUNK_W[c]], ACT.Copy, scale=HS).then_inc(h_hi, 1)
                            if c == 1 and not (s == 1 and last_pair):
                                for i in range(PIECES[stage_]):
                                    weights_hi(stage_, pair, s + 1, i)

                if experts > 2:
                    with act.Fori(0, experts // 2 - 1) as pair:
                        body(pair, False)
                if middle:
                    middle()
                body(experts // 2 - 1, True)

            ln_root("g0")
            take_transposes("g0")
            first_weights_hi("f0", 0)
            act.wait_ge(deg_max, 1)
            nc.scalar.activation(dsq[:, :], dinv[:, :], ACT.Sqrt).then_inc(deg_root, 1)
            ln_root("f0")
            take_transposes("t_f0", split=True)
            first_weights_hi("f0", 1)
            gate_exp("f0", 1.0)

            def head_norms():
                act.wait_ge(all_done, 1)
                nc.scalar.activation(nB, nB, ACT.Sqrt).then_inc(cnt_root, 1)

            ffn("f0", ACT.Gelu_apprx_tanh, head_norms)
            ln_root("g1")
            first_weights_hi("f1", 0)
            ln_root("f1")
            take_transposes("t_f1", split=True)
            first_weights_hi("f1", 1)
            gate_exp("f1", 1.0)
            ffn("f1", ACT.Gelu)
            ln_root("g2")
            take_transposes("g2")
            i = H0["g2"] + T_ITEMS
            for k2 in range(KD):
                for c in range(NC):
                    take(i, uT3[:, k2, c * CW:c * CW + CHUNK_W[c]], CHUNK_W[c], ACT.Identity, bias=bnode[:, k2:k2 + 1])
                    i += 1
            for c in range(NC):
                for g, (j0, j1) in enumerate(J_GROUPS):
                    act.wait_ge(blk_raw, 2 * c + g + 1)
                    b = block3[c % 2][:, j0:j1, 0:CHUNK_W[c]]
                    nc.scalar.activation(b, b, ACT.Exp).then_inc(blk_exp, 1)
            for g in (0, 1):
                ln_root("m_a", (g,))
                ln_root("m_b", (g,))
            take_transposes("mamba_in")
            i = H0["mamba_in"] + T_ITEMS
            own(nc.scalar.activation(mA[:, :], malog[:, :], ACT.Exp))
            own(nc.scalar.activation(mA[:, :], mA[:, :], ACT.Copy, scale=-1.0))

            def silu_of(d):
                act.wait_ge(conv_done, d + 1)
                nc.scalar.activation(xs[:, d, :], cacc[d % 2], ACT.Silu, bias=mcb[:, d:d + 1]).then_inc(xs_ready, 1)

            act.wait_ge(pad_zero, 1)
            for d in range(DB):
                if d >= 2:
                    silu_of(d - 2)
                for c in range(NC):
                    take(i, xcp[d % 2][:, TAPS - 1 + c * MW:TAPS - 1 + (c + 1) * MW], MW)
                    i += 1
            silu_of(DB - 2)
            silu_of(DB - 1)
            for c in range(NC):
                take(i, dbc[:, c * MW:(c + 1) * MW], MW, rows_=48)
                i += 1
            act.wait_ge(h_used, H_BANKS + i)
            mA3 = mA[:, :].rearrange("p (n d) -> p n d", d=DB)
            PER = 4
            act.wait_ge(w_split, 2 + PIECE0["f2"])
            with act.Fori(0, NC) as c:
                i = H0["mamba_scan"]
                act.wait_ge(m_y, c + 1)
                nc.scalar.activation(dbcc[:, :], dbc[:, bass.ds(c * MW, MW)], ACT.Copy).then_inc(m_dbc, 1)
                for d in range(DB):
                    act.wait_ge(h_done, c * (2 * DB) + (i + d + 1))
                    nc.scalar.activation(delta[:, d, :], psH[(i + d) % H_BANKS][:, 0:MW], ACT.Abs, bias=mdb[:, d:d + 1])\
                        .then_inc(act_chain, 1)
                    nc.scalar.activation(u[:, d, :], psH[(i + d) % H_BANKS][:, 0:MW], ACT.Relu, bias=mdb[:, d:d + 1])\
                        .then_inc(h_used, 1)
                act.wait_ge(act_chain, c * DB + (n_own[0] + DB))
                nc.scalar.activation(delta[:, :, :], delta[:, :, :], ACT.Exp, scale=-1.0).then_inc(sp_ready, 1)
                for d in range(DB):
                    act.wait_ge(h_done, c * (2 * DB) + (i + DB + d + 1))
                    nc.scalar.activation(zg[:, d, :], psH[(i + DB + d) % H_BANKS][:, 0:MW], ACT.Silu).then_inc(h_used, 1)
                def take_bc(n):
                    act.wait_ge(m_bc, c * DS + (n + 1))
                    if n >= 4:
                        act.wait_ge(m_hc, c * DS + (n - 1))
                        act.wait_ge(m_hcp, c * DS + (n - 1))
                    nc.scalar.activation(Bs[n % 4], psB[n % 2][:, 0:MW], ACT.Copy)
                    nc.scalar.activation(Cs[n % 4], psC[n % 2][:, 0:MW], ACT.Copy).then_inc(m_bcs, 1)

                take_bc(0)
                take_bc(1)
                act.wait_ge(m_chain, c * M_CHAIN + (len(LOG1P) + 1))
                for n in range(DS):
                    if n + 2 < DS:
                        take_bc(n + 2)
                    act.wait_ge(m_hc, c * DS + (n + 1))
                    for d in reversed(range(DB)):
                        last = nc.scalar.activation(dA[n % 2][:, d, :], delta[:, d, :], ACT.Exp, scale=mA3[:, n, d:d + 1])
                    last.then_inc(m_dA, 1)
            n_own[0] += NC * DB
            act.wait_ge(m_y, NC + 1)
            act.wait_ge(m_hcp, NC * DS + 2)
            first_weights_hi("f2", 0)
            ln_root("f2")
            take_transposes("t_f2", split=True)
            first_weights_hi("f2", 1)
            ffn("f2", ACT.Relu)
            ln_root("g3")
            take_transposes("g3")
            for c in range(NC):
                take(H0["g3"] + T_ITEMS + c, row[:, c * CW:c * CW + CHUNK_W[c]], CHUNK_W[c])
            for c in range(NC):
                for g, (j0, j1) in enumerate(J_GROUPS):
                    act.wait_ge(blk_raw, 2 * (NC + c) + g + 1)
                    b = block3[c % 2][:, j0:j1, 0:CHUNK_W[c]]
                    nc.scalar.activation(b, b, ACT.Exp, scale=-1.0).then_inc(blk_exp, 1)
                if c == 1:
                    act.wait_ge(za_ready, 1)
                    nc.scalar.activation(sig[:, :, :], sig[:, :, :], ACT.Sigmoid).then_inc(za_sig, 1)
            first_weights_hi("f3", 0)
            act.wait_ge(fin_ready, 1)
            nc.scalar.activation(XB[:, 0:2 * TPC, :], XB[:, 0:2 * TPC, :], ACT.Sigmoid).then_inc(fin_sig, 1)
            ln_root("f3", (0,))
            act.wait_ge(fin_ready, 2)
            nc.scalar.activation(XB[:, 2 * TPC:NT - 1, :], XB[:, 2 * TPC:NT - 1, :], ACT.Sigmoid)
            nc.scalar.activation(XB[0:LAST, NT - 1, :], XB[0:LAST, NT - 1, :], ACT.Sigmoid).then_inc(fin_sig, 1)
            ln_root("f3", (1,))
            take_transposes("t_f3", split=True)
            first_weights_hi("f3", 1)
            gate_exp("f3", 1.0 / 2.5)
            ffn("f3", ACT.Gelu_apprx_tanh)

        @block.vector
        def _(dve):
            dve.sem_inc(y_used, Y_BANKS)
            dve.sem_inc(w_split, 2)
            dve.sem_inc(h_split, 2)
            dve.sem_inc(m_y, 1)
            dve.sem_inc(m_hc, 2)
            n_own = [0]
            tt, ts, stt = nc.vector.tensor_tensor, nc.vector.tensor_scalar, nc.vector.scalar_tensor_tensor

            def own(ins):
                n_own[0] += 1
                ins.then_inc(chain, 1)
                dve.wait_ge(chain, n_own[0])

            def ln_stats(src, g):
                i = slice(GROUPS[g][0], GROUPS[g][-1] + 1)
                for t in GROUPS[g]:
                    last = nc.vector.bn_stats(st[:, t, :], src[:, t, 0:D])
                own(last)
                for t in GROUPS[g]:
                    last = nc.vector.bn_aggr(mv[:, t, :], st[:, t, :])
                own(last)
                ts(var[:, i], mv[:, i, 1], EPS, None, ALU.add).then_inc(ln_var, 1)

            n_ln = [0]

            def ln_apply(src, dst, g):
                i = slice(GROUPS[g][0], GROUPS[g][-1] + 1)
                n_ln[0] += 1
                dve.wait_ge(ln_std, n_ln[0])
                own(nc.vector.reciprocal(rstd[:, i], std[:, i]))
                for t in GROUPS[g]:
                    last = ts(dst[:, t, 0:D], src[:, t, 0:D], mv[:, t, 0:1], rstd[:, t:t + 1], ALU.subtract, ALU.mult)
                last.then_inc(ln_out, 1)
                dve.wait_ge(ln_out, n_ln[0])

            def layernorm(src, dst):
                for g in (0, 1):
                    ln_stats(src, g)
                    ln_apply(src, dst, g)

            def finish_and_normalise(consume, settled, src, dst):
                for t in GROUPS[0]:
                    consume(t)
                settled(GROUPS[0][-1])
                ln_stats(src, 0)
                consume(GROUPS[1][0])
                ln_apply(src, dst, 0)
                for t in GROUPS[1][1:]:
                    consume(t)
                settled(NT - 1)
                ln_stats(src, 1)
                ln_apply(src, dst, 1)

            def weights_lo(stage_, pair, e, i):
                n = PIECES[stage_]
                dve.wait_ge(w_hi, pair * (2 * n) + (PIECE0[stage_] + e * n + i + 1))
                hi, lo = (wparts[:, e % 2, i // (n // 2), q, i % (n // 2) * PIECE:(i % (n // 2) + 1) * PIECE] for q in range(2))
                stt(lo, stage[:, i % 2, :], WS, hi, ALU.mult, ALU.subtract).then_inc(w_split, 1)

            def first_weights_lo(stage_, half):
                for i in range(2 * half, min(2 * half + 2, PIECES[stage_])):
                    weights_lo(stage_, 0, 0, i)

            def split_x(stage_):
                dve.wait_ge(x_hi, T_ITEMS * (X_SPLIT0[stage_] + 1))
                dve.wait_ge(h_used, H_BANKS + H0["t_" + stage_] + T_ITEMS)
                stt(x16[1], xT3, XS, x16[0], ALU.mult, ALU.subtract).then_inc(x_split, 1)

            def all_taken(stage):
                dve.wait_ge(y_used, Y_BANKS + Y0[stage])

            def wide(ap, n, w):
                return ap.unsqueeze(1).broadcast_to([P, n, w])

            def gating(stage, biased, renorm):
                g = GATE[stage]
                dve.wait_ge(g_done, g + 1)
                logits = psM[0][:, 0:NT * 8].rearrange("p (t e) -> p t e", e=8)

                def per_token(v):
                    return v[:, :].unsqueeze(2).broadcast_to([P, NT, 8])

                if biased:
                    own(tt(lg[:, :, :], logits, wide(bgate[:, :], NT, 8), ALU.add))
                else:
                    own(nc.vector.tensor_copy(lg[:, :, :], logits))
                own(nc.vector.tensor_reduce(gmx[:, :], lg[:, :, :], AX_X, ALU.max))
                tt(lg[:, :, :], lg[:, :, :], per_token(gmx), ALU.subtract).then_inc(g_shift, 1)
                dve.wait_ge(g_exp, g + 1)
                own(nc.vector.tensor_reduce(gsum[:, :], pr[:, :, :], AX_X, ALU.add))
                own(nc.vector.reciprocal(gsum[:, :], gsum[:, :]))
                own(tt(pr[:, :, :], pr[:, :, :], per_token(gsum), ALU.mult))
                c0, c1 = (v.rearrange("p (t e f) -> p t e f", e=8, f=8) for v in cmp)
                pf = pr[:, :, :].unsqueeze(2).broadcast_to([P, NT, 8, 8])
                pe_ = pr[:, :, :].unsqueeze(3).broadcast_to([P, NT, 8, 8])
                tt(c0, pf, pe_, ALU.is_gt)
                own(tt(c1, pf, pe_, ALU.is_equal))
                c1f = cmp[1].rearrange("p (t e) -> p t e", e=64)
                own(tt(c1f, c1f, wide(before[:, :], NT, 64), ALU.mult))
                own(tt(cmp[0], cmp[0], cmp[1], ALU.add))
                own(nc.vector.tensor_reduce(rank[:, :, :], c0, AX_X, ALU.add))
                own(stt(gates[:, :, 0:8], rank[:, :, :], 2.0, pr[:, :, :], ALU.is_lt, ALU.mult))
                if renorm:
                    own(nc.vector.tensor_reduce(gsum[:, :], gates[:, :, 0:8], AX_X, ALU.add))
                    own(nc.vector.reciprocal(gsum[:, :], gsum[:, :]))
                    own(tt(gates[:, :, 0:8], gates[:, :, 0:8], per_token(gsum), ALU.mult))

            def ffn(stage_, tail, middle=None):
                experts, fb = FFN[stage_]
                y0, h0, i0 = Y0[stage_], H0[stage_], ITEM0[stage_]
                own(ts(gates_s[:, :, :], gates[:, :, :], 1.0 / (HS * WS), None, ALU.mult))

                def body(pair, last_pair):
                    def gate(g, s, t):
                        return g[0:rows(t), t, bass.ds(pair * 2 + s, 1)]

                    def split(s, c):
                        w = CHUNK_W[c]
                        for f in range(0, fb, 2):
                            i = (s * NC + c) * fb + f
                            raw = hraw[:, (i0 + i) % 4:(i0 + i) % 4 + 2, 0:w]
                            hi, lo = (hT[fb][(s * NC + c) % 2][q][:, f:f + 2, 0:w] for q in range(2))
                            dve.wait_ge(h_hi, pair * (NC * fb) + ((i0 + i) // 2 + 1))
                            stt(lo, raw, HS, hi, ALU.mult, ALU.subtract).then_inc(h_split, 1)

                    def add_bias(s, t):
                        i = s * NT + t
                        if t == 0:
                            dve.wait_ge(b_in[s], pair * (2 * DMA) + 2 * DMA * (LOADS0[stage_] // 2 + 1))
                        dve.wait_ge(y_used, pair * (2 * NT) + (Y_BANKS + y0 + i - NT + 1))
                        stt(x[0:rows(t), t, :], b2[0:rows(t), s, :], gate(gates, s, t), x[0:rows(t), t, :],
                            ALU.mult, ALU.add).then_inc(b_added, 1)

                    def add_product(s, t):
                        i = s * NT + t
                        dve.wait_ge(b_added, pair * (2 * NT) + (LOADS0[stage_] * NT + i + 1))
                        dve.wait_ge(y_done, pair * (2 * NT) + (y0 + i + 2))
                        stt(x[0:rows(t), t, :], psY[(y0 + i) % Y_BANKS][0:rows(t), 0:D], gate(gates_s, s, t), x[0:rows(t), t, :],
                            ALU.mult, ALU.add).then_inc(y_used, 1)
                        if t < PIECES[stage_] and not (s == 1 and last_pair):
                            weights_lo(stage_, pair, s + 1, t)

                    def add_both(t):
                        add_bias(1, t)
                        add_product(1, t)

                    order = [(s, c) for s in range(2) for c in range(NC)]
                    for n, (s, c) in enumerate(order):
                        s1, c1 = order[n - 1]
                        added = CHUNK_T[c1] if n and not (last_pair and n == len(order) - 1) else ()
                        for t in added:
                            add_bias(s1, t)
                        split(s, c)
                        for t in added:
                            add_product(s1, t)
                    if last_pair:
                        tail(add_both, lambda t: dve.wait_ge(y_used, Y_BANKS + y0 + (experts - 1) * NT + t + 1))
                    else:
                        for add in (add_bias, add_product):
                            for t in CHUNK_T[NC - 1]:
                                add(1, t)

                if experts > 2:
                    with dve.Fori(0, experts // 2 - 1) as pair:
                        body(pair, False)
                if middle:
                    middle()
                body(experts // 2 - 1, True)

            nc.vector.memset(ones[:, :], 1.0).then_inc(ones_set, 1)
            nc.vector.memset(gates[:, :, :], 1.0)
            own(nc.vector.memset(xn[:, :, D:XC], 1.0))
            dve.wait_ge(x_in, DMA)
            layernorm(x, xn)
            own(nc.vector.memset(deg[:, :], 0.0))
            dve.wait_ge(adj_in[0], DMA)
            ts(cnt, adj3[:, 0, :], 0.0, None, ALU.is_gt)
            own(nc.vector.tensor_copy(mxp, adj3[:, 0, :]))
            for j in range(1, NT):
                dve.wait_ge(adj_in[j], DMA)
                stt(cnt, adj3[:, j, :], 0.0, cnt, ALU.is_gt, ALU.add)
                own(tt(mxp[0:rows(j), :], mxp[0:rows(j), :], adj3[0:rows(j), j, :], ALU.max))
            dve.sem_inc(part_done, 1)
            first_weights_lo("f0", 0)
            dve.wait_ge(deg_done, 1)
            nc.vector.tensor_copy(deg[:, 0:NT - 1], psM[1][:, 0:NT - 1])
            own(nc.vector.tensor_copy(deg[0:LAST, NT - 1:NT], psM[1][0:LAST, NT - 1:NT]))
            ts(dinv[:, :], deg[:, :], 1e-35, None, ALU.max).then_inc(deg_max, 1)
            dve.wait_ge(deg_root, 1)
            own(nc.vector.reciprocal(dinv[:, :], dsq[:, :]))
            own(stt(dinv[:, :], deg[:, :], 0.0, dinv[:, :], ALU.is_gt, ALU.mult))
            y = Y0["g0"]
            for t in range(NT):
                dve.wait_ge(y_done, y + 2)
                ts(V3[0:rows(t), t, 0:D], psY[y % Y_BANKS][0:rows(t), 0:D], dinv[0:rows(t), t:t + 1], None, ALU.mult).then_inc(y_used, 1)
                y += 1
            dve.wait_ge(y_used, Y_BANKS + y)
            dve.sem_inc(v_ready, 1)
            y_g0 = y
            dve.wait_ge(const_in, DMA * N_CONST)

            def take0(t):
                r, y = rows(t), y_g0 + t
                dve.wait_ge(y_done, y + 2)
                stt(tmp[0:r, t % 2, :], psY[y % Y_BANKS][0:r, 0:D], dinv[0:r, t:t + 1], bias0[0:r, :], ALU.mult, ALU.add).then_inc(y_used, 1)
                dve.wait_ge(y_used, Y_BANKS + y + 1)
                own(stt(x[0:r, t, :], tmp[0:r, t % 2, :], 0.0, x[0:r, t, :], ALU.max, ALU.add))

            finish_and_normalise(take0, lambda t: None, x, xn)
            split_x("f0")
            first_weights_lo("f0", 1)
            gating("f0", False, False)

            def normalise_x(add, settled):
                done = TPC

                def consume(t):
                    if t >= done:
                        add(t)

                finish_and_normalise(consume, settled, x, xn)

            def head_norms():
                dve.wait_ge(all_done, 2)
                dve.wait_ge(cnt_root, 1)
                own(ts(nB, nB, 1e-12, None, ALU.max))
                own(nc.vector.reciprocal(nB, nB))

            ffn("f0", normalise_x, head_norms)
            own(nc.vector.memset(xn[:, :, D:XC], 1.0))

            def block1(c):
                w = CHUNK_W[c]
                for j0, j1 in J_GROUPS:
                    b, av = block3[c % 2][:, j0:j1, 0:w], adj3[:, j0:j1, c * CW:c * CW + w]
                    own(stt(b, av, 0.0, wide(nB[:, c * CW:c * CW + w], j1 - j0, w), ALU.is_gt, ALU.mult))
                    tt(b, b, av, ALU.add).then_inc(blk, 1)

            def take1(t):
                r, y = rows(t), Y0["g1"] + t
                if t == TPC:
                    block1(2)
                    first_weights_lo("f1", 0)
                dve.wait_ge(y_done, y + 2)
                own(nc.vector.reciprocal(rc[0:r, t % 2, 0:1], psY[y % Y_BANKS][0:r, D:D + 1]))
                stt(x[0:r, t, :], psY[y % Y_BANKS][0:r, 0:D], rc[0:r, t % 2, 0:1], x[0:r, t, :], ALU.mult, ALU.add).then_inc(y_used, 1)

            block1(0)
            block1(1)
            finish_and_normalise(take1, lambda t: dve.wait_ge(y_used, Y_BANKS + Y0["g1"] + t + 1), x, V3)
            split_x("f1")
            first_weights_lo("f1", 1)
            gating("f1", True, False)
            ffn("f1", normalise_x)
            dve.wait_ge(gk_in, DMA)
            own(tt(g2k[:, 0], g2k[:, 0], g2k[:, 1], ALU.add))
            own(tt(g2k[:, 0], g2k[:, 0], g2k[:, 2], ALU.add))
            own(tt(g2k[:, 0], g2k[:, 0], g2k[:, 3], ALU.add))
            ts(g2k[:, 0], g2k[:, 0], 0.25, None, ALU.mult).then_inc(kmean, 1)
            own(ts(row[:, 0:N], row[:, 0:N], -1.0, 1.0, ALU.mult, ALU.add))
            own(ts(row[:, 0:N], row[:, 0:N], NEG, None, ALU.mult))

            def block2(c):
                w = CHUNK_W[c]
                for j0, j1 in J_GROUPS:
                    b = block3[c % 2][:, j0:j1, 0:w]
                    own(ts(b, adj3[:, j0:j1, c * CW:c * CW + w], -1.0, 1.0, ALU.mult, ALU.add))
                    stt(b, b, NEG, wide(row[:, c * CW:c * CW + w], j1 - j0, w), ALU.mult, ALU.subtract).then_inc(blk_raw, 1)

            def take2(t):
                if t == TPC:
                    block2(2)
                r, y = rows(t), Y0["g2"] + NT + t
                dve.wait_ge(y_done, y + 2)
                own(nc.vector.reciprocal(rc[0:r, 0, 0:1], psY[y % Y_BANKS][0:r, D:D + 1]))
                ts(tmp[0:r, 0, :], psY[y % Y_BANKS][0:r, 0:D], rc[0:r, 0, 0:1], 0.0, ALU.mult, ALU.max).then_inc(y_used, 1)
                dve.wait_ge(y_used, Y_BANKS + y + 1)
                own(tt(x[0:r, t, :], tmp[0:r, 0, :], x[0:r, t, :], ALU.add))

            block2(0)
            own(nc.vector.memset(V3[:, :, D:D + 1], 1.0))
            y = Y0["g2"]
            for t in range(NT):
                dve.wait_ge(y_done, y + 2)
                nc.vector.tensor_copy(V3[0:rows(t), t, 0:D], psY[y % Y_BANKS][0:rows(t), 0:D]).then_inc(y_used, 1)
                y += 1
            dve.wait_ge(y_used, Y_BANKS + y)
            dve.sem_inc(v_ready, 1)
            block2(1)
            for t in GROUPS[0]:
                take2(t)
            ln_stats(x, 0)
            take2(GROUPS[1][0])
            ln_apply(x, xn, 0)
            ln_stats(xn, 0)
            for t in GROUPS[1][1:]:
                take2(t)
            ln_apply(xn, xh, 0)
            ln_stats(x, 1)
            ln_apply(x, xn, 1)
            ln_stats(xn, 1)
            ln_apply(xn, xh, 1)
            for i in range(2):
                last = nc.vector.memset(xcp[i][:, 0:TAPS - 1], 0.0)
            last.then_inc(pad_zero, 1)
            own(nc.vector.memset(carry[:, :], 0.0))
            for d in range(DB):
                dve.wait_ge(h_used, H_BANKS + H0["mamba_in"] + T_ITEMS + (d + 1) * NC)
                if d >= 2:
                    dve.wait_ge(xs_ready, d - 1)
                acc, src = cacc[d % 2], xcp[d % 2]
                own(ts(acc, src[:, 0:MN], mcw[:, d, 0:1], None, ALU.mult))
                for k in range(1, TAPS):
                    ins = stt(acc, src[:, k:k + MN], mcw[:, d, k:k + 1], acc, ALU.mult, ALU.add)
                    if k < TAPS - 1:
                        own(ins)
                    else:
                        ins.then_inc(conv_done, 1)
            dve.wait_ge(w_hi, PIECE0["f2"])
            with dve.Fori(0, NC) as c:
                m = [0]

                def fire(ins):
                    m[0] += 1
                    ins.then_inc(m_chain, 1)
                    return m[0]

                def mown(ins):
                    dve.wait_ge(m_chain, c * M_CHAIN + fire(ins))

                dve.wait_ge(sp_ready, c + 1)
                poly = dBx[0]
                mown(ts(poly, delta[:, :, :], LOG1P[-1], None, ALU.mult))
                for coef in LOG1P[-2::-1]:
                    mown(stt(poly, poly, coef, delta[:, :, :], ALU.add, ALU.mult))
                mown(tt(delta[:, :, :], poly, u[:, :, :], ALU.add))
                mown(tt(u[:, :, :], delta[:, :, :], xs[:, :, bass.ds(c * MW, MW)], ALU.mult))

                def times_b(n):
                    dve.wait_ge(m_bcs, c * DS + (n + 3))
                    return fire(tt(dBx[n % 2][:, 0:VB, :], u[:, 0:VB, :], wide(Bs[n % 4], VB, MW), ALU.mult))

                def scan(n, d):
                    return nc.vector.tensor_tensor_scan(hS[n % 2][:, d, :], dA[n % 2][:, d, :], dBx[n % 2][:, d, :],
                                                        carry[:, n * DB + d:n * DB + d + 1], ALU.mult, ALU.add)

                own_b = times_b(0)
                for n in range(DS):
                    dve.wait_ge(m_dA, c * DS + (n + 1))
                    dve.wait_ge(m_db, c * DS + (n + 1))
                    dve.wait_ge(m_hcp, c * DS + (n + 1))
                    for d in range(VB, DB):
                        last = scan(n, d)
                    last.then_inc(m_h, 1)
                    dve.wait_ge(m_chain, c * M_CHAIN + own_b)
                    for d in range(VB):
                        last = scan(n, d)
                    own_h = fire(last)
                    if n + 1 < DS:
                        own_b = times_b(n + 1)
                    dve.wait_ge(m_h, c * DS + (n + 1))
                    dve.wait_ge(m_chain, c * M_CHAIN + own_h)
                    nc.vector.tensor_copy(carry[:, n * DB:(n + 1) * DB], hS[n % 2][:, :, MW - 1])
                    if n >= 2:
                        dve.wait_ge(m_acc, c * DS + (n - 1))
                    tt(hC[n % 2][:, 0:VB, :], hS[n % 2][:, 0:VB, :], wide(Cs[n % 4], VB, MW), ALU.mult).then_inc(m_hc, 1)
                dve.wait_ge(m_acc, c * DS + DS)
                for d in range(DB):
                    last = stt(dBx[0][:, d, :], xs[:, d, bass.ds(c * MW, MW)], mds[:, d:d + 1],
                               psH[(H0["mamba_scan"] + d) % H_BANKS][:, 0:MW], ALU.mult, ALU.add)
                mown(last)
                tt(xs[:, :, bass.ds(c * MW, MW)], dBx[0], zg[:, :, :], ALU.mult).then_inc(m_y, 1)
                assert m[0] == M_CHAIN
            first_weights_lo("f2", 0)

            def take_m(t):
                r, y = rows(t), Y0["mamba_out"] + t
                dve.wait_ge(y_done, y + 2)
                tt(xh[0:r, t, :], psY[y % Y_BANKS][0:r, 0:D], xh[0:r, t, :], ALU.add).then_inc(y_used, 1)

            finish_and_normalise(take_m, lambda t: dve.wait_ge(y_used, Y_BANKS + Y0["mamba_out"] + t + 1), xh, xh)
            own(nc.vector.memset(gates[:, :, 0:2], 0.5))
            own(tt(x[:, :, :], x[:, :, :], xn[:, :, 0:D], ALU.add))
            split_x("f2")
            first_weights_lo("f2", 1)
            ffn("f2", normalise_x)
            own(nc.vector.memset(xn[:, :, D:XC], 1.0))
            dve.wait_ge(a_done, 1)
            nc.vector.tensor_copy(g3r[:, :, D:D + 2], psM[0][:, 0:4].rearrange("p (k n) -> p k n", k=KD)).then_inc(a_used, 1)
            y = Y0["g3"]
            for t in range(NT):
                dve.wait_ge(y_done, y + 2)
                nc.vector.tensor_copy(V3[0:rows(t), t, 0:D + 2], psY[y % Y_BANKS][0:rows(t), 0:D + 2]).then_inc(y_used, 1)
                y += 1
            for t in range(NT):
                r = rows(t)
                dve.wait_ge(y_done, y + 2)
                nc.vector.tensor_copy(xn[0:r, t, 0:D], psY[y % Y_BANKS][0:r, 0:D])
                nc.vector.tensor_copy(xn[0:r, t, D + 1:XC], psY[y % Y_BANKS][0:r, D + 1:XC]).then_inc(y_used, 1)
                y += 1
            dve.wait_ge(y_used, Y_BANKS + y)
            dve.sem_inc(v_ready, 1)
            dve.wait_ge(h_used, H_BANKS + H0["g3"] + T_ITEMS + NC)
            dve.wait_ge(adj_again, DMA)

            def block3_(c):
                w = CHUNK_W[c]
                for j0, j1 in J_GROUPS:
                    b = block3[c % 2][:, j0:j1, 0:w]
                    own(tt(b, wide(row[:, c * CW:c * CW + w], j1 - j0, w), xn[:, j0:j1, D + 1:D + 2].broadcast_to([P, j1 - j0, w]), ALU.add))
                    stt(b, b, 0.01, b, ALU.mult, ALU.max).then_inc(blk_raw, 1)

            def mask3(c):
                w = CHUNK_W[c]
                for g, (j0, j1) in enumerate(J_GROUPS):
                    b = block3[c % 2][:, j0:j1, 0:w]
                    dve.wait_ge(blk_exp, 2 * (NC + c) + g + 1)
                    stt(b, adj3[:, j0:j1, c * CW:c * CW + w], 0.0, b, ALU.not_equal, ALU.mult).then_inc(blk, 1)

            ya = y

            def take_b(tiles):
                for t in tiles:
                    r, y = rows(t), ya + t
                    dve.wait_ge(y_done, y + 2)
                    tt(sig[0:r, t, :], psY[y % Y_BANKS][0:r, D:D + 2], xn[0:r, t, D + 2:D + 4], ALU.add)
                    tt(XB[0:r, t, :], psY[y % Y_BANKS][0:r, 0:D], bias3[0:r, :], ALU.add).then_inc(y_used, 1)

            def take_a(t):
                r, y = rows(t), ya + NT + t
                dve.wait_ge(y_done, y + 2)
                ts(XB[0:r, t, :], XB[0:r, t, :], sig[0:r, t, 1:2], None, ALU.mult)
                own(ts(rc[0:r, t % 2, 0:1], psY[y % Y_BANKS][0:r, D:D + 1], EPS, None, ALU.add))
                own(nc.vector.reciprocal(rc[0:r, t % 2, 1:2], rc[0:r, t % 2, 0:1]))
                own(ts(rc[0:r, t % 2, 0:1], rc[0:r, t % 2, 1:2], sig[0:r, t, 0:1], None, ALU.mult))
                stt(XB[0:r, t, :], psY[y % Y_BANKS][0:r, 0:D], rc[0:r, t % 2, 0:1], XB[0:r, t, :], ALU.mult, ALU.add).then_inc(y_used, 1)

            own(nc.vector.memset(sig[:, :, :], 0.0))
            block3_(0)
            take_b(range(0, 3))
            mask3(0)
            take_b(range(3, 6))
            block3_(1)
            take_b(range(6, NT))
            dve.wait_ge(y_used, Y_BANKS + ya + NT)
            own(tt(sig[:, :, :], sig[:, :, :], wide(bab[:, :], NT, 2), ALU.add))
            dve.sem_inc(za_ready, 1)
            mask3(1)
            dve.wait_ge(za_sig, 1)
            for t in range(0, TPC):
                take_a(t)
            block3_(2)
            take_a(TPC)
            mask3(2)
            first_weights_lo("f3", 0)
            for t in range(TPC + 1, 2 * TPC):
                take_a(t)
            dve.wait_ge(y_used, Y_BANKS + ya + NT + 2 * TPC)
            dve.sem_inc(fin_ready, 1)
            take_a(2 * TPC)
            dve.wait_ge(fin_sig, 1)
            own(tt(x[:, 0:2 * TPC, :], x[:, 0:2 * TPC, :], XB[:, 0:2 * TPC, :], ALU.add))
            ln_stats(x, 0)
            for t in GROUPS[1][1:]:
                take_a(t)
            dve.wait_ge(y_used, Y_BANKS + Y0["t_f3"])
            dve.sem_inc(fin_ready, 1)
            ln_apply(x, V3, 0)
            dve.wait_ge(fin_sig, 2)
            tt(x[:, 2 * TPC:NT - 1, :], x[:, 2 * TPC:NT - 1, :], XB[:, 2 * TPC:NT - 1, :], ALU.add)
            own(tt(x[0:LAST, NT - 1, :], x[0:LAST, NT - 1, :], XB[0:LAST, NT - 1, :], ALU.add))
            ln_stats(x, 1)
            ln_apply(x, V3, 1)
            split_x("f3")
            first_weights_lo("f3", 1)
            gating("f3", False, True)

            def add_rest(add, settled):
                for t in range(TPC, NT):
                    add(t)

            ffn("f3", add_rest)


N_CONST = 12
LOG1P = (1.0, -0.4999950151678741, 0.33319271342508366, -0.24844369892516138, 0.1911143108072622,
         -0.13674769705756462, 0.07836166802050314, -0.02958850739350184, 0.005253457797072649)
M_CHAIN = len(LOG1P) + 2 + 2 * DS + 1


def kernel(**inputs):
    import numpy as np
    import concourse.bacc as bacc
    from concourse.bass_utils import run_bass_kernel_spmd

    i = {k: np.asarray(v) for k, v in inputs.items()}
    f = np.float32

    def blocks(w, axis=0):
        return np.moveaxis(w.reshape(w.shape[0] // P, P, *w.shape[1:]), 0, 1)

    def experts(w):
        e, r, n = w.shape
        return w.reshape(e, r // P, P, n).transpose(0, 2, 1, 3).reshape(e, P, r // P * n)

    def hidden_bias(b):
        e, n = b.shape
        return b.reshape(e, n // P, P).transpose(0, 2, 1)

    xp = np.zeros((NT * P, D), f)
    xp[:N] = i["x"]
    adj = np.zeros((NT * P, N), f)
    adj[:N] = i["adj"].T
    g3sa = i["L3_gnn_W_sa"]
    wa, wb = i["L3_gnn_Wa"][0], i["L3_gnn_Wb"][0]
    arrays = {
        "x": blocks(xp), "adj": blocks(adj),
        "ident": np.eye(P, dtype=f),         "before": np.tile(np.tril(np.ones((8, 8), f), -1).reshape(1, 64), (P, 1)),
        "wgate": np.stack([blocks(i["L0_ffn_Wg"]), blocks(i["L1_ffn_gate_w"].T), blocks(i["L3_ffn_Wr"])], 1),
        "bnode": blocks(i["L2_gnn_b_node"]),
        "mcw": blocks(i["L2_ffn_conv_w"][:, 0, :]), "mcb": blocks(i["L2_ffn_conv_b"]), "mdb": blocks(i["L2_ffn_dt_proj_b"]),
        "mds": blocks(i["L2_ffn_D_skip"]),
        "malog": blocks(i["L2_ffn_A_log"]).transpose(0, 2, 1).reshape(P, DB * DS),
        "bias0": i["L0_gnn_b"].reshape(1, D), "bias3": i["L3_gnn_b_gcnb"].reshape(1, D),
        "bgate": i["L1_ffn_gate_b"].reshape(1, 8), "bab": np.concatenate([i["L3_gnn_ba"], i["L3_gnn_bb"]]).reshape(1, 2),
        "g0w": blocks(i["L0_gnn_W"]), "g2n": blocks(i["L2_gnn_W_node"]),
        "g2k": np.stack([blocks(k) for k in i["L2_gnn_K"]], 1),
        "g3sa": blocks(g3sa), "g3t": blocks(g3sa.T), "g3a": blocks(i["L3_gnn_a_sa"].reshape(2, D).T),
        "g3x": blocks(np.stack([wa[D:], wb[D:]], 1)),
        "g3l": blocks(np.concatenate([i["L3_gnn_W_gcnb"], wa[:D, None], wb[:D, None]], 1)),
        "mwin": blocks(i["L2_ffn_in_proj_w"].T), "mwx": blocks(i["L2_ffn_x_proj_w"].T),
        "mwdt": i["L2_ffn_dt_proj_w"].T, "mwo": blocks(i["L2_ffn_out_proj_w"].T),
        "w1_0": experts(i["L0_ffn_W1"]), "w2_0": experts(i["L0_ffn_W2"]), "b1_0": hidden_bias(i["L0_ffn_b1"]), "b2_0": i["L0_ffn_b2"],
        "w1_1": experts(np.concatenate([i["L1_ffn_rw1"], i["L1_ffn_sw1"]]).transpose(0, 2, 1)),
        "w2_1": experts(np.concatenate([i["L1_ffn_rw2"], i["L1_ffn_sw2"]]).transpose(0, 2, 1)),
        "b1_1": hidden_bias(np.concatenate([i["L1_ffn_rb1"], i["L1_ffn_sb1"]])),
        "b2_1": np.concatenate([i["L1_ffn_rb2"], i["L1_ffn_sb2"]]),
        "w1_2": experts(i["L2_ffn_moe_w1"].transpose(0, 2, 1)), "w2_2": experts(i["L2_ffn_moe_w2"].transpose(0, 2, 1)),
        "b1_2": hidden_bias(i["L2_ffn_moe_b1"]), "b2_2": i["L2_ffn_moe_b2"],
        "w1_3": experts(i["L3_ffn_W1"]), "w2_3": experts(i["L3_ffn_W2"]), "b1_3": hidden_bias(i["L3_ffn_b1"]), "b2_3": i["L3_ffn_b2"],
    }
    nc = bacc.Bacc("TRN2", target_bir_lowering=False, num_devices=1)
    feed, args = {}, {}
    for name, v in arrays.items():
        v = np.ascontiguousarray(v)
        feed[f"in_{name}"] = v
        args[name] = nc.dram_tensor(f"in_{name}", v.shape, F32, kind="ExternalInput").ap()
    out = nc.dram_tensor("out", (N, D), F32, kind="ExternalOutput").ap()
    build(nc, args, out)
    r = run_bass_kernel_spmd(nc, [feed], core_ids=[0])
    return r.results[0]["out"]
```
